# Optimizing a Trainium2 kernel written in Bass

```python
import numpy as np
import jax
import jax.numpy as jnp

def _softmax(x, axis=-1):
    return jax.nn.softmax(x, axis=axis)

def _gelu(x):
    return jax.nn.gelu(x, approximate=True)

def _silu(x):
    return jax.nn.silu(x)

def _sigmoid(x):
    return jax.nn.sigmoid(x)

def _layernorm(x, axis=-1, eps=1e-05):
    m = jnp.mean(x, axis=axis, keepdims=True)
    v = jnp.var(x, axis=axis, keepdims=True)
    return (x - m) / jnp.sqrt(v + eps)

def _scatter_add(tgt, idx, src, axis=0):
    return tgt.at[idx].add(src)

def _segment_sum(src, seg, n):
    return jax.ops.segment_sum(src, seg, n)
kernel_name = 'mk_adj_preln_d1_adj_r2_e445af'

def setup_inputs(seed: int=0):
    np.random.seed(seed)
    _w = jnp.asarray

    def _rec_inputs():
        import jax
        import jax.numpy as jnp
        _gk = jax.random.key(seed)
        x = 7.22e-05 + 1 * jax.random.normal(jax.random.fold_in(_gk, 1), (16, 512, 128), jnp.float32)
        _w = (1.0 + jnp.arange(512, dtype=jnp.float32)) ** (-0.5)
        _w = _w / _w.mean()
        _pij = jnp.clip(0.015625 * _w[:, None] * _w[None, :], 0.0, 1.0)
        _a = jax.random.uniform(jax.random.fold_in(_gk, 2), (512, 512)) < _pij
        _a = jnp.logical_or(_a, jnp.swapaxes(_a, -1, -2))
        _a = jnp.logical_or(_a, jnp.eye(512, dtype=bool))
        _af = _a.astype(jnp.float32)
        _af = _af * jax.random.uniform(jax.random.fold_in(_gk, 3), (512, 512), jnp.float32, 0.05, 0.000976562)
        adj = _af
        return (x, adj)
    x, adj = _rec_inputs()

    def _L0_gnn_setup():
        import jax, jax.numpy as jnp
        import numpy as np
        N_STEPS = 8
        SPATIAL_SCALE = 1.0
        key = jax.random.key(seed)
        ks = jax.random.split(key, 6)
        B, N, D = (32, 512, 128)
        x = jax.random.normal(ks[0], (B, N, D), dtype=jnp.float32)
        adj_mx = jax.random.uniform(ks[1], (N, N), dtype=jnp.float32) / N
        alpha_train = jnp.ones((N,), dtype=jnp.float32)
        w = jnp.eye(D, dtype=jnp.float32) + 0.01 * jax.random.normal(ks[2], (D, D), dtype=jnp.float32)
        d = jax.random.uniform(ks[3], (D,), dtype=jnp.float32)
        fc_in_w = jax.random.normal(ks[4], (D, D), dtype=jnp.float32) * (1.0 / np.sqrt(D))
        fc_in_b = jnp.zeros((D,), dtype=jnp.float32)
        return {'x': x, 'adj_mx': adj_mx, 'alpha_train': alpha_train, 'w': w, 'd': d, 'fc_in_w': fc_in_w, 'fc_in_b': fc_in_b, 'vt': 0}
    _L0_gnn_all = _L0_gnn_setup()
    _L0_gnn_in = {k: v for k, v in _L0_gnn_all.items() if k in ('alpha_train', 'w', 'd', 'fc_in_w', 'fc_in_b')}
    del _L0_gnn_all
    return {'x': x, 'adj': adj, 'L0_gnn_alpha_train': _L0_gnn_in['alpha_train'], 'L0_gnn_w': _L0_gnn_in['w'], 'L0_gnn_d': _L0_gnn_in['d'], 'L0_gnn_fc_in_w': _L0_gnn_in['fc_in_w'], 'L0_gnn_fc_in_b': _L0_gnn_in['fc_in_b']}

def reference(x, adj, L0_gnn_alpha_train, L0_gnn_w, L0_gnn_d, L0_gnn_fc_in_w, L0_gnn_fc_in_b):
    import jax
    import jax.numpy as jnp

    def _L0_gnn_ref(x, adj_mx, alpha_train, w, d, fc_in_w, fc_in_b, vt):
        import jax, jax.numpy as jnp
        import numpy as np
        N_STEPS = 8
        SPATIAL_SCALE = 1.0
        x0 = jax.lax.stop_gradient(x)
        h = jnp.einsum('bnd,ed->bne', x, fc_in_w) + fc_in_b
        alph = jax.nn.sigmoid(alpha_train)[:, None]
        d_clamped = jnp.clip(d, 0.0, 1.0)
        w_eff = w * d_clamped @ w.T
        dt = jnp.float32(SPATIAL_SCALE / N_STEPS)

        def euler_step(h, _):
            ax = jnp.einsum('nm,bmd->bnd', adj_mx, h)
            f = alph * 0.5 * (ax - h) + h @ w_eff - h + x0
            return (h + dt * f, None)
        h, _ = jax.lax.scan(euler_step, h, None, length=N_STEPS)
        return h
    h = jnp.maximum(_layernorm(x, axis=-1), 0.0)
    x = x + _L0_gnn_ref(h, adj, L0_gnn_alpha_train, L0_gnn_w, L0_gnn_d, L0_gnn_fc_in_w, L0_gnn_fc_in_b, 0)
    return x

_drawn_inputs = setup_inputs


def setup_inputs(seed=0):
    import zlib

    import numpy as np

    out = dict(_drawn_inputs(seed))
    spreads = {'L0_gnn_alpha_train': (1.0, 0.2), 'L0_gnn_fc_in_b': (0.0, 0.1)}
    factors = {}
    for name, (base, spread) in spreads.items():
        noise = np.random.default_rng([zlib.crc32(name.encode()), seed]).standard_normal(out[name].shape)
        drawn = base * np.exp(spread * noise) if base else spread * noise
        out[name] = jnp.asarray(drawn.astype(out[name].dtype))
    for name, factor in factors.items():
        out[name] = (out[name] * factor).astype(out[name].dtype)
    return out
```

```python
from contextlib import ExitStack
from math import comb

import concourse.bass as bass
from concourse import mybir

ALU = mybir.AluOpType
ACT = mybir.ActivationFunctionType
AX = mybir.AxisListType
F32 = mybir.dt.float32
F32R = mybir.dt.float32r

P = 128
STEPS = 8
DT = 1.0 / STEPS
EPS = 1e-5
GB = 4


def build(nc, x, adj, alpha, w, d, fc_w, fc_b, out):
    B, N, D = x.shape
    T = N // P
    G = B // GB
    assert D == P and N == T * P and GB * D == 512 and N == 512 and B == G * GB
    place = {3 * (2 - c) + s: (s, c) for s in range(3) for c in range(3)}

    x_dram = x.rearrange("b (p t) d -> b p (t d)", t=T)
    out_dram = out.rearrange("(g b) (p t) d -> g t p b d", b=GB, t=T)
    adj_dram = adj.rearrange("(p t) m -> t p m", t=T)

    with ExitStack() as ctx:
        def sb(name, shape, dt=F32):
            return ctx.enter_context(nc.sbuf_tensor(name, shape, dt))

        def psum(name, shape):
            return ctx.enter_context(nc.psum_tensor(name, shape, F32))

        def sem(name):
            return ctx.enter_context(nc.semaphore(name))

        def pair(name, shape):
            return sb(name + "_hi", shape, F32R), sb(name + "_lo", shape, F32R)

        xs = sb("xs", [P, B, T, D])
        ident = sb("ident", [P, P])
        dt_ident = sb("dt_ident", [P, P])
        sel = sb("sel", [6, 4])
        adj_sb = sb("adj_sb", [P, T, N])
        alpha_sb = sb("alpha_sb", [P, T])
        exp_alpha = sb("exp_alpha", [P, T])
        gate = sb("gate", [P, T])
        diag = sb("diag", [P, T])
        L = sb("L", [P, T, T, P])
        L_hi, L_lo = pair("L", [P, T, T, P])
        LT_hi, LT_lo = pair("LT", [P, T, N])
        L2T_hi, L2T_lo = pair("L2T", [P, T, N])
        L3T_hi, L3T_lo = pair("L3T", [P, T, N])
        w_sb = sb("w_sb", [P, P])
        d_sb = sb("d_sb", [P, 1])
        d_clip = sb("d_clip", [P, 1])
        wT = sb("wT", [P, P])
        wTd = sb("wTd", [P, P])
        fc_sb = sb("fc_sb", [P, P])
        b_sb = sb("b_sb", [P, 1])
        R = sb("R", [P, STEPS + 1, P])
        C = sb("C", [P, 3, 3 * P])
        C_hi, C_lo = pair("C", [P, 3, 3 * P])
        u_col = sb("u_col", [P, T, 3])
        u_split = sb("u_split", [P, T, P], F32R)
        u_rows = sb("u_rows", [6, 4, N])
        g_col = sb("g_col", [P, 3, 6])
        g_rows = sb("g_rows", [6, 3, P])
        bias = sb("bias", [P, T * D])
        stats = sb("stats", [P, T, 6])
        halves, halves_apart, apart_sq = sb("halves", [P, T, 2]), sb("halves_apart", [P, T]), sb("apart_sq", [P, T])
        mean = sb("mean", [P, T])
        var_eps, std, rstd0, newton, rstd = (sb(n, [P, T]) for n in ("var_eps", "std", "rstd0", "newton", "rstd"))
        normed = [sb(f"normed{n}", [P, T, D]) for n in range(2)]
        x0 = [pair(f"x0_{n}", [P, T, D]) for n in range(2)]
        srcT = [[pair(f"src{s}T_{n}", [P, N]) for s in range(3)] for n in range(2)]
        q2_hi, q2_lo = pair("q2", [P, T, GB, D])
        r1 = adj_sb[:].rearrange("p t (b d) -> p t b d", b=GB)
        y1_sum = [sb(f"y1_sum{n}", [P, GB * D]) for n in range(2)]
        y1_hi, y1_lo = (a[:].rearrange("p t c q -> p t (c q)") for a in (L_hi, L_lo))

        psW = psum("psW", [P, T, 512])
        psZ = psum("psZ", [P, 2, 512])
        psT = psum("psT", [P, 512])
        psS = psum("psS", [P, 512])

        adj_in = [sem(f"adj_in{t}") for t in range(T)]
        alpha_in, w_in, d_in, fc_in, b_in = (sem(n) for n in ("alpha_in", "w_in", "d_in", "fc_in", "b_in"))
        x_in = [sem(f"x_in{j}") for j in range(GB)]
        zeros_set, ident_set, sel_set, dt_ident_set = (sem(n) for n in ("zeros_set", "ident_set", "sel_set", "dt_ident_set"))
        exp_set, gate_chain, gate_set = sem("exp_set"), sem("gate_chain"), sem("gate_set")
        L_scaled, L_set, L_hi_set, L_lo_set = sem("L_scaled"), sem("L_set"), sem("L_hi_set"), sem("L_lo_set")
        LT_done, LT_hi_set, LT_lo_set = sem("LT_done"), sem("LT_hi_set"), sem("LT_lo_set")
        L2T_done, L2T_hi_set, L2T_lo_set = sem("L2T_done"), sem("L2T_hi_set"), sem("L2T_lo_set")
        L3T_done, L3T_hi_set, L3T_lo_set = sem("L3T_done"), sem("L3T_hi_set"), sem("L3T_lo_set")
        d_set, wT_done, wT_set, wTd_set = sem("d_set"), sem("wT_done"), sem("wT_set"), sem("wTd_set")
        R_done, R_set = sem("R_done"), sem("R_set")
        FR_done, FR_set, C_sum, C_hi_set, C_lo_set = sem("FR_done"), sem("FR_set"), sem("C_sum"), sem("C_hi_set"), sem("C_lo_set")
        g_done, g_set, g_rows_done, g_rows_set = sem("g_done"), sem("g_set"), sem("g_rows_done"), sem("g_rows_set")
        u_chain, u_split_set, u_rows_done, u_rows_set = sem("u_chain"), sem("u_split_set"), sem("u_rows_done"), sem("u_rows_set")
        u_cols_done, bias_done, bias_set = sem("u_cols_done"), sem("bias_done"), sem("bias_set")
        ln_chain, std_set, normed_set, x0_hi_set, x0_lo_set = sem("ln_chain"), sem("std_set"), sem("normed_set"), sem("x0_hi_set"), sem("x0_lo_set")
        xT_done, xT_hi_set, xT_lo_set = sem("xT_done"), sem("xT_hi_set"), sem("xT_lo_set")
        z_done, z_hi_set, z_lo_set = sem("z_done"), sem("z_hi_set"), sem("z_lo_set")
        c_done, c_hi_set, c_lo_set, bias_added = sem("c_done"), sem("c_hi_set"), sem("c_lo_set"), sem("bias_added")
        y1_done, y1_sum_set, y1_hi_set, y1_lo_set = sem("y1_done"), sem("y1_sum_set"), sem("y1_hi_set"), sem("y1_lo_set")
        y_done, y_set, stored = sem("y_done"), sem("y_set"), sem("stored")

        LN = 9
        LN_VAR = 5

        block = ctx.enter_context(nc.Block())

        @block.sync
        def _(sp):
            for t in range(T):
                sp.dma_start(adj_sb[:, t, :], adj_dram[t]).then_inc(adj_in[t], 16)
            for j in range(GB):
                sp.dma_start(xs[:, j, :, :], x_dram[j]).then_inc(x_in[j], 16)
            with sp.Fori(1, G) as g:
                for j in range(GB):
                    sp.wait_ge(x_in[j], 16 * g)
                    sp.dma_start(xs[:, bass.ds(GB * g + j, 1), :, :],
                                 x_dram[bass.ds(GB * g + j, 1)].rearrange("o p n -> (o p) n")).then_inc(x_in[j], 16)
            with sp.Fori(0, G) as g:
                for t in range(T):
                    sp.wait_ge(y_set, T * g + t + 1)
                    sp.dma_start(out_dram[bass.ds(g, 1), t].rearrange("o p b d -> (o p) b d"),
                                 xs[:, bass.ds(GB * g, GB), t, :]).then_inc(stored, 16)
            sp.wait_ge(stored, 16 * G * T)

        @block.gpsimd
        def _(pool):
            nc.gpsimd.memset(ident[:], 0.0).then_inc(zeros_set, 1)
            nc.gpsimd.memset(sel[:], 0.0).then_inc(zeros_set, 1)
            pool.wait_ge(zeros_set, 2)
            nc.gpsimd.affine_select(out=ident[:], in_=ident[:], compare_op=ALU.not_equal, fill=1.0, base=0,
                                    pattern=[[-1, P]], channel_multiplier=1).then_inc(ident_set, 1)
            nc.gpsimd.affine_select(out=sel[:], in_=sel[:], compare_op=ALU.not_equal, fill=1.0, base=0,
                                    pattern=[[-1, 4]], channel_multiplier=1).then_inc(sel_set, 1)
            pool.wait_ge(sel_set, 1)
            nc.gpsimd.affine_select(out=sel[:], in_=sel[:], compare_op=ALU.not_equal, fill=1.0, base=-3,
                                    pattern=[[-1, 4]], channel_multiplier=1).then_inc(sel_set, 1)
            pool.wait_ge(ident_set, 1)
            nc.gpsimd.tensor_scalar(dt_ident[:], ident[:], DT, 0.0, ALU.mult, ALU.add).then_inc(dt_ident_set, 1)
            for t in range(T):
                pool.wait_ge(L_hi_set, t + 1)
                nc.gpsimd.tensor_tensor(L_lo[:, t], L[:, t], L_hi[:, t].bitcast(F32), ALU.subtract).then_inc(L_lo_set, 1)

            def group(g):
                for j in range(GB):
                    pool.wait_ge(c_lo_set, 2 * (GB * g + j) + 2)
                    xb = xs[:, bass.ds(GB * g + j, 1), :, :].rearrange("p o t d -> p (o t d)")
                    nc.gpsimd.tensor_tensor(xb, xb, bias[:], ALU.add).then_inc(bias_added, 1)
                for t in range(T):
                    pool.wait_ge(y1_hi_set, T * g + t + 1)
                    nc.gpsimd.tensor_tensor(y1_lo[:, t], y1_sum[t % 2][:], y1_hi[:, t].bitcast(F32),
                                            ALU.subtract).then_inc(y1_lo_set, 1)

            pool.wait_ge(bias_set, 1)
            with pool.Fori(0, G) as g:
                group(g)

        @block.scalar
        def _(act):
            act.dma_start(alpha_sb[:], alpha.rearrange("(p t) -> p t", t=T)).then_inc(alpha_in, 16)
            act.dma_start(w_sb[:], w).then_inc(w_in, 16)
            act.dma_start(d_sb[:], d.rearrange("(p o) -> p o", o=1)).then_inc(d_in, 16)
            act.dma_start(fc_sb[:], fc_w).then_inc(fc_in, 16)
            act.dma_start(b_sb[:], fc_b.rearrange("(p o) -> p o", o=1)).then_inc(b_in, 16)
            act.wait_ge(alpha_in, 16)
            nc.scalar.activation(exp_alpha[:], alpha_sb[:], ACT.Exp, scale=-1.0).then_inc(exp_set, 1)
            for n, (lo, hi) in enumerate(((1, 2), (2, 3), (3, 5), (5, 9))):
                act.wait_ge(R_done, n + 1)
                nc.scalar.activation(R[:, lo:hi, :], psS[:, 0:(hi - lo) * P], ACT.Copy).then_inc(R_set, 1)

            def split_L():
                for t in range(T):
                    act.wait_ge(L_set, t + 1)
                    nc.scalar.activation(L_hi[:, t], L[:, t], ACT.Copy).then_inc(L_hi_set, 1)

            def power_hi(done, count, hi, hi_set, t):
                act.wait_ge(done, count)
                nc.scalar.activation(hi[:, t, :], psW[:, t, :], ACT.Copy).then_inc(hi_set, 1)

            def fr_scaled(n):
                act.wait_ge(FR_done, n + 1)
                for j in range(3 * n, 3 * n + 3):
                    s, c = place[8 - j]
                    ins = nc.scalar.activation(C[:, s, c * P:(c + 1) * P], psS[:, (j - 3 * n) * P:(j - 3 * n + 1) * P],
                                               ACT.Copy, scale=float(comb(8, j)))
                ins.then_inc(FR_set, 1)

            def deviation(i):
                act.wait_ge(ln_chain, LN * i + LN_VAR)
                nc.scalar.activation(std[:], var_eps[:], ACT.Sqrt).then_inc(std_set, 1)

            def x0_hi(i, n):
                act.wait_ge(normed_set, i + 1)
                if not (isinstance(i, int) and i < 2):
                    act.wait_ge(z_done, 2 * i - 2)
                nc.scalar.activation(x0[n][0][:], normed[n][:], ACT.Relu).then_inc(x0_hi_set, 1)

            def xT_hi(i, n):
                act.wait_ge(xT_done, i + 1)
                nc.scalar.activation(srcT[n][0][0][:], psT[:], ACT.Relu).then_inc(xT_hi_set, 1)

            def z_hi(i, n, s):
                act.wait_ge(z_done, 2 * i + s)
                nc.scalar.activation(srcT[n][s][0][:], psZ[:, s - 1, :], ACT.Copy).then_inc(z_hi_set, 1)

            def c_hi(i, j):
                for h in range(2):
                    act.wait_ge(c_done, 2 * i + h + 1)
                    nc.scalar.activation(q2_hi[:, 2 * h:2 * h + 2, j, :], psW[:, 2 * h:2 * h + 2, 0:P], ACT.Copy)
                    nc.scalar.activation(r1[:, 2 * h:2 * h + 2, j, :], psW[:, 2 * h:2 * h + 2, P:2 * P],
                                         ACT.Copy).then_inc(c_hi_set, 1)

            def y1_hi_part(g):
                for t in range(T):
                    act.wait_ge(y1_sum_set, T * g + t + 1)
                    nc.scalar.activation(y1_hi[:, t], y1_sum[t % 2][:], ACT.Copy).then_inc(y1_hi_set, 1)

            def group(g, last=False):
                c_hi(GB * g, 0)
                xT_hi(GB * g + 2, 0)
                z_hi(GB * g + 2, 0, 1)
                z_hi(GB * g + 2, 0, 2)
                c_hi(GB * g + 1, 1)
                xT_hi(GB * g + 3, 1)
                z_hi(GB * g + 3, 1, 1)
                z_hi(GB * g + 3, 1, 2)
                if not last:
                    deviation(GB * g + 4)
                c_hi(GB * g + 2, 2)
                if not last:
                    x0_hi(GB * g + 4, 0)
                    deviation(GB * g + 5)
                c_hi(GB * g + 3, 3)
                if not last:
                    x0_hi(GB * g + 5, 1)
                    deviation(GB * g + 6)
                    xT_hi(GB * g + 4, 0)
                    z_hi(GB * g + 4, 0, 1)
                    z_hi(GB * g + 4, 0, 2)
                    x0_hi(GB * g + 6, 0)
                    deviation(GB * g + 7)
                y1_hi_part(g)
                if not last:
                    xT_hi(GB * g + 5, 1)
                    z_hi(GB * g + 5, 1, 1)
                    z_hi(GB * g + 5, 1, 2)
                    x0_hi(GB * g + 7, 1)

            split_L()
            deviation(0)
            for t in range(T):
                power_hi(LT_done, 1, LT_hi, LT_hi_set, t)
            fr_scaled(0)
            x0_hi(0, 0)
            deviation(1)
            for t in range(T):
                power_hi(L2T_done, t + 1, L2T_hi, L2T_hi_set, t)
            xT_hi(0, 0)
            z_hi(0, 0, 1)
            fr_scaled(1)
            fr_scaled(2)
            x0_hi(1, 1)
            deviation(2)
            for t in range(T):
                power_hi(L3T_done, t + 1, L3T_hi, L3T_hi_set, t)
            z_hi(0, 0, 2)
            x0_hi(2, 0)
            deviation(3)
            act.wait_ge(C_sum, STEPS)
            nc.scalar.activation(C_hi[:], C[:], ACT.Copy).then_inc(C_hi_set, 1)
            xT_hi(1, 1)
            z_hi(1, 1, 1)
            z_hi(1, 1, 2)
            x0_hi(3, 1)
            with act.Fori(0, G - 1) as g:
                group(g)
            group(G - 1, last=True)

        @block.tensor
        def _(pe):
            def product(o, terms):
                for n, ((a_hi, a_lo), (b_hi, b_lo)) in enumerate(terms):
                    nc.tensor.matmul(o, a_hi, b_hi, start=(n == 0), stop=False)
                    nc.tensor.matmul(o, a_hi, b_lo, start=False, stop=False)
                    ins = nc.tensor.matmul(o, a_lo, b_hi, start=False, stop=(n == len(terms) - 1))
                return ins

            def power_tile(b_hi, b_lo, t):
                return product(psW[:, t, :], [((L_hi[:, k, t, :], L_lo[:, k, t, :]),
                                               (b_hi[:, k, :], b_lo[:, k, :])) for k in range(T)])

            def transpose_x(i, n):
                pe.wait_ge(normed_set, i + 1)
                if not (isinstance(i, int) and i < 1):
                    pe.wait_ge(xT_lo_set, i)
                for t in range(T):
                    ins = nc.tensor.transpose(psT[:, t * P:(t + 1) * P], normed[n][:, t, :], ident[:])
                ins.then_inc(xT_done, 1)

            def make_z(i, n, s):
                if s == 1:
                    pe.wait_ge(x0_lo_set, i + 1)
                if not (isinstance(i, int) and i < 1):
                    pe.wait_ge(z_lo_set, 2 * i - 2 + s)
                mT = (LT_hi, LT_lo) if s == 1 else (L2T_hi, L2T_lo)
                product(psZ[:, s - 1, :], [((x0[n][0][:, m, :], x0[n][1][:, m, :]),
                                            (mT[0][:, m, :], mT[1][:, m, :])) for m in range(T)]).then_inc(z_done, 1)

            def make_c(i, j, n):
                pe.wait_ge(xT_lo_set, i + 1)
                pe.wait_ge(z_lo_set, 2 * i + 2)
                for t in range(T):
                    if t % 2 == 0 and j > 0:
                        pe.wait_ge(c_lo_set, 2 * i - 1 + t // 2)
                    ins = product(psW[:, t, 0:3 * P], [((srcT[n][s][0][:, t * P:(t + 1) * P],
                                                        srcT[n][s][1][:, t * P:(t + 1) * P]),
                                                       (C_hi[:, s, :], C_lo[:, s, :])) for s in range(3)])
                    if t % 2 == 1:
                        ins.then_inc(c_done, 1)

            def make_y1(g):
                pe.wait_ge(c_lo_set, 2 * GB * g + 2 * GB)
                for t in range(T):
                    product(psW[:, t, :], [((L3T_hi[:, m, t * P:(t + 1) * P], L3T_lo[:, m, t * P:(t + 1) * P]),
                                            (q2_hi[:, m], q2_lo[:, m])) for m in range(T)]).then_inc(y1_done, 1)

            def make_y(g):
                pe.wait_ge(y1_lo_set, T * g + T)
                for t in range(T):
                    product(psW[:, t, :], [((L3T_hi[:, m, t * P:(t + 1) * P], L3T_lo[:, m, t * P:(t + 1) * P]),
                                            (y1_hi[:, m], y1_lo[:, m])) for m in range(T)]).then_inc(y_done, 1)

            def group(g, last=False):
                make_c(GB * g, 0, 0)
                transpose_x(GB * g + 2, 0)
                make_z(GB * g + 2, 0, 1)
                make_z(GB * g + 2, 0, 2)
                make_c(GB * g + 1, 1, 1)
                transpose_x(GB * g + 3, 1)
                make_z(GB * g + 3, 1, 1)
                make_z(GB * g + 3, 1, 2)
                make_c(GB * g + 2, 2, 0)
                make_c(GB * g + 3, 3, 1)
                if not last:
                    transpose_x(GB * g + 4, 0)
                    make_z(GB * g + 4, 0, 1)
                    make_z(GB * g + 4, 0, 2)
                make_y1(g)
                if not last:
                    transpose_x(GB * g + 5, 1)
                    make_z(GB * g + 5, 1, 1)
                    make_z(GB * g + 5, 1, 2)
                make_y(g)
                if not last:
                    pe.wait_ge(y_set, T * g + T)

            def u_times(b_hi, b_lo):
                for n, (b, m) in enumerate([(b, m) for b in (b_hi, b_lo) for m in range(T)]):
                    ins = nc.tensor.matmul(psS[:], u_split[:, m, :], b[:, m, :], start=(n == 0), stop=(n == 2 * T - 1))
                ins.then_inc(u_rows_done, 1)

            def u_columns(row_block):
                for t in range(T):
                    ins = nc.tensor.matmul(psS[:, 4 * t:4 * t + 4], u_rows[:, row_block, t * P:(t + 1) * P], sel[:],
                                           start=True, stop=True)
                ins.then_inc(u_cols_done, 1)

            pe.wait_ge(ident_set, 1)
            pe.wait_ge(w_in, 16)
            nc.tensor.transpose(psS[:, 0:P], w_sb[:], ident[:]).then_inc(wT_done, 1)
            pe.wait_ge(wTd_set, 1)
            nc.tensor.matmul(psS[:, 0:P], wTd[:], wT[:], start=True, stop=True).then_inc(R_done, 1)
            for n, (by, lo, hi) in enumerate(((1, 1, 2), (2, 1, 3), (4, 1, 5))):
                pe.wait_ge(R_set, n + 1)
                nc.tensor.matmul(psS[:, 0:(hi - lo) * P], R[:, by, :], R[:, lo:hi, :], start=True,
                                 stop=True).then_inc(R_done, 1)
            for t in range(T):
                pe.wait_ge(L_set, t + 1)
                for m in range(T):
                    ins = nc.tensor.transpose(psW[:, m, t * P:(t + 1) * P], L[:, t, m, :], ident[:])
            ins.then_inc(LT_done, 1)
            pe.wait_ge(fc_in, 16)
            pe.wait_ge(R_set, 4)
            nc.tensor.matmul(psS[:, 0:P], fc_sb[:], ident[:], start=True, stop=True)
            nc.tensor.matmul(psS[:, P:3 * P], fc_sb[:], R[:, 1:3, :], start=True, stop=True).then_inc(FR_done, 1)
            pe.wait_ge(L_lo_set, T)
            pe.wait_ge(LT_lo_set, T)
            for t in range(T):
                power_tile(LT_hi, LT_lo, t).then_inc(L2T_done, 1)
            transpose_x(0, 0)
            make_z(0, 0, 1)
            pe.wait_ge(FR_set, 1)
            nc.tensor.matmul(psS[:, 0:3 * P], fc_sb[:], R[:, 3:6, :], start=True, stop=True).then_inc(FR_done, 1)
            pe.wait_ge(L2T_lo_set, T)
            power_tile(L2T_hi, L2T_lo, 0).then_inc(L3T_done, 1)
            pe.wait_ge(FR_set, 2)
            nc.tensor.matmul(psS[:, 0:3 * P], fc_sb[:], R[:, 6:9, :], start=True, stop=True).then_inc(FR_done, 1)
            power_tile(L2T_hi, L2T_lo, 1).then_inc(L3T_done, 1)
            pe.wait_ge(FR_set, 3)
            pe.wait_ge(b_in, 16)
            for j in range(1, STEPS + 1):
                ins = nc.tensor.matmul(psS[:, j:j + 1], R[:, j, :], b_sb[:], start=True, stop=True)
            ins.then_inc(g_done, 1)
            power_tile(L2T_hi, L2T_lo, 2).then_inc(L3T_done, 1)
            pe.wait_ge(g_set, 1)
            for n in range(3):
                ins = nc.tensor.matmul(psS[0:6, n * P:(n + 1) * P], g_col[:, n, :], ident[:], start=True, stop=True)
            ins.then_inc(g_rows_done, 1)
            power_tile(L2T_hi, L2T_lo, 3).then_inc(L3T_done, 1)
            pe.wait_ge(g_rows_set, 1)
            pe.wait_ge(u_split_set, 1)
            u_times(LT_hi, LT_lo)
            make_z(0, 0, 2)
            pe.wait_ge(u_rows_set, 1)
            pe.wait_ge(sel_set, 2)
            u_columns(0)
            transpose_x(1, 1)
            make_z(1, 1, 1)
            pe.wait_ge(u_split_set, 2)
            for t in range(T):
                ins = nc.tensor.matmul(psS[0:6, t * P:(t + 1) * P], u_split[:, t, 0:6].bitcast(F32), ident[:],
                                       start=True, stop=True)
            ins.then_inc(u_rows_done, 1)
            make_z(1, 1, 2)
            pe.wait_ge(u_rows_set, 2)
            pe.wait_ge(L3T_lo_set, T)
            u_times(L3T_hi, L3T_lo)
            pe.wait_ge(u_rows_set, 3)
            u_columns(2)
            pe.wait_ge(u_split_set, 3)
            u_times(L3T_hi, L3T_lo)
            pe.wait_ge(u_rows_set, 4)
            for t in range(T):
                for n in range(3):
                    ins = nc.tensor.matmul(psS[:, t * P:(t + 1) * P], u_rows[:, n + 1, t * P:(t + 1) * P],
                                           g_rows[:, n, :], start=(n == 0), stop=(n == 2))
            ins.then_inc(bias_done, 1)
            pe.wait_ge(C_lo_set, 1)
            with pe.Fori(0, G - 1) as g:
                group(g)
            group(G - 1, last=True)

        @block.vector
        def _(dve):
            def lo_part(lo, full, hi):
                return nc.vector.tensor_tensor(lo, full, hi.bitcast(F32), ALU.subtract)

            def power_lo(hi_set, hi, lo, lo_set, t):
                dve.wait_ge(hi_set, t + 1)
                lo_part(lo[:, t, :], psW[:, t, :], hi[:, t, :]).then_inc(lo_set, 1)

            def statistics(i, j, g):
                dve.wait_ge(x_in[j], 16 * g + 16)
                xb = xs[:, bass.ds(i, 1), :, :]
                for t in range(T):
                    ins = nc.vector.bn_stats(stats[:, t, :], xb[:, :, t, :].rearrange("p o d -> p (o d)"))
                ins.then_inc(ln_chain, 1)
                dve.wait_ge(ln_chain, LN * i + 1)
                nc.vector.tensor_tensor(halves[:], stats[:, :, 1:3], stats[:, :, 4:6], ALU.add)
                nc.vector.tensor_tensor(halves_apart[:], stats[:, :, 1], stats[:, :, 4],
                                        ALU.subtract).then_inc(ln_chain, 1)
                dve.wait_ge(ln_chain, LN * i + 2)
                nc.vector.tensor_scalar(mean[:], halves[:, :, 0], 0.5, None, ALU.mult)
                nc.vector.tensor_tensor(apart_sq[:], halves_apart[:], halves_apart[:], ALU.mult).then_inc(ln_chain, 1)
                dve.wait_ge(ln_chain, LN * i + 3)
                nc.vector.scalar_tensor_tensor(apart_sq[:], apart_sq[:], D / 4.0, halves[:, :, 1], ALU.mult,
                                               ALU.add).then_inc(ln_chain, 1)
                dve.wait_ge(ln_chain, LN * i + 4)
                nc.vector.tensor_scalar(var_eps[:], apart_sq[:], 1.0 / D, EPS, ALU.mult, ALU.add).then_inc(ln_chain, 1)

            def normalize(i, n):
                dve.wait_ge(std_set, i + 1)
                nc.vector.reciprocal(rstd0[:], std[:]).then_inc(ln_chain, 1)
                dve.wait_ge(ln_chain, LN * i + 6)
                nc.vector.tensor_tensor(newton[:], var_eps[:], rstd0[:], ALU.mult).then_inc(ln_chain, 1)
                dve.wait_ge(ln_chain, LN * i + 7)
                nc.vector.scalar_tensor_tensor(newton[:], newton[:], -0.5, rstd0[:], ALU.mult, ALU.mult).then_inc(ln_chain, 1)
                dve.wait_ge(ln_chain, LN * i + 8)
                nc.vector.scalar_tensor_tensor(rstd[:], newton[:], 1.5, rstd0[:], ALU.add, ALU.mult).then_inc(ln_chain, 1)
                dve.wait_ge(ln_chain, LN * i + 9)
                xb = xs[:, bass.ds(i, 1), :, :]
                if not (isinstance(i, int) and i < 2):
                    dve.wait_ge(xT_done, i - 1)
                    dve.wait_ge(x0_hi_set, i - 1)
                for t in range(T):
                    ins = nc.vector.tensor_scalar(normed[n][:, t, :], xb[:, :, t, :].rearrange("p o d -> p (o d)"),
                                                  mean[:, t:t + 1], rstd[:, t:t + 1], ALU.subtract, ALU.mult)
                ins.then_inc(normed_set, 1)

            def relu_lo(lo, full, hi):
                return nc.vector.scalar_tensor_tensor(lo, full, 0.0, hi.bitcast(F32), ALU.max, ALU.subtract)

            def x0_lo(i, n):
                dve.wait_ge(x0_hi_set, i + 1)
                relu_lo(x0[n][1][:], normed[n][:], x0[n][0][:]).then_inc(x0_lo_set, 1)

            def xT_lo(i, n):
                dve.wait_ge(xT_hi_set, i + 1)
                relu_lo(srcT[n][0][1][:], psT[:], srcT[n][0][0][:]).then_inc(xT_lo_set, 1)

            def z_lo(i, n, s):
                dve.wait_ge(z_hi_set, 2 * i + s)
                lo_part(srcT[n][s][1][:], psZ[:, s - 1, :], srcT[n][s][0][:]).then_inc(z_lo_set, 1)

            def c_lo(i, j):
                for h in range(2):
                    dve.wait_ge(c_hi_set, 2 * i + h + 1)
                    t2 = slice(2 * h, 2 * h + 2)
                    lo_part(q2_lo[:, t2, j, :], psW[:, t2, 0:P], q2_hi[:, t2, j, :])
                    xb = xs[:, bass.ds(i, 1), t2, :].rearrange("p o t d -> p (o t) d")
                    nc.vector.tensor_tensor(xb, psW[:, t2, 2 * P:3 * P], xb, ALU.add).then_inc(c_lo_set, 1)

            def y1_part(g):
                for t in range(T):
                    dve.wait_ge(y1_done, T * g + t + 1)
                    if t >= 2:
                        dve.wait_ge(y1_lo_set, T * g + t - 1)
                    nc.vector.tensor_tensor(y1_sum[t % 2][:], psW[:, t, :], r1[:, t].rearrange("p b d -> p (b d)"),
                                            ALU.add).then_inc(y1_sum_set, 1)

            def y_part(g):
                dve.wait_ge(bias_added, GB * g + GB)
                for t in range(T):
                    dve.wait_ge(y_done, T * g + t + 1)
                    xg = xs[:, bass.ds(GB * g, GB), t, :]
                    nc.vector.tensor_tensor(xg, psW[:, t, :].rearrange("p (b d) -> p b d", b=GB), xg,
                                            ALU.add).then_inc(y_set, 1)

            def group(g, last=False):
                c_lo(GB * g, 0)
                xT_lo(GB * g + 2, 0)
                z_lo(GB * g + 2, 0, 1)
                z_lo(GB * g + 2, 0, 2)
                c_lo(GB * g + 1, 1)
                xT_lo(GB * g + 3, 1)
                z_lo(GB * g + 3, 1, 1)
                z_lo(GB * g + 3, 1, 2)
                if not last:
                    statistics(GB * g + 4, 0, g + 1)
                c_lo(GB * g + 2, 2)
                if not last:
                    normalize(GB * g + 4, 0)
                    statistics(GB * g + 5, 1, g + 1)
                    x0_lo(GB * g + 4, 0)
                c_lo(GB * g + 3, 3)
                if not last:
                    normalize(GB * g + 5, 1)
                    statistics(GB * g + 6, 2, g + 1)
                    x0_lo(GB * g + 5, 1)
                    xT_lo(GB * g + 4, 0)
                    z_lo(GB * g + 4, 0, 1)
                    z_lo(GB * g + 4, 0, 2)
                    normalize(GB * g + 6, 0)
                    statistics(GB * g + 7, 3, g + 1)
                    x0_lo(GB * g + 6, 0)
                y1_part(g)
                if not last:
                    xT_lo(GB * g + 5, 1)
                    z_lo(GB * g + 5, 1, 1)
                    z_lo(GB * g + 5, 1, 2)
                    normalize(GB * g + 7, 1)
                    x0_lo(GB * g + 7, 1)
                y_part(g)

            def split_u(n):
                dve.wait_ge(u_chain, n)
                nc.vector.tensor_copy(u_split[:, :, 0:3], u_col[:]).then_inc(u_chain, 1)
                dve.wait_ge(u_chain, n + 1)
                lo_part(u_split[:, :, 3:6], u_col[:], u_split[:, :, 0:3]).then_inc(u_split_set, 1)

            def keep_u_rows(row_block, done):
                dve.wait_ge(u_rows_done, done)
                nc.vector.tensor_copy(u_rows[:, row_block, :], psS[0:6, :]).then_inc(u_rows_set, 1)

            dve.wait_ge(exp_set, 1)
            nc.vector.tensor_scalar(exp_alpha[:], exp_alpha[:], 1.0, None, ALU.add).then_inc(gate_chain, 1)
            dve.wait_ge(gate_chain, 1)
            nc.vector.reciprocal(gate[:], exp_alpha[:]).then_inc(gate_chain, 1)
            dve.wait_ge(gate_chain, 2)
            nc.vector.tensor_scalar(gate[:], gate[:], DT * 0.5, None, ALU.mult).then_inc(gate_chain, 1)
            dve.wait_ge(gate_chain, 3)
            nc.vector.tensor_scalar(diag[:], gate[:], -1.0, 1.0 - DT, ALU.mult, ALU.add).then_inc(gate_set, 1)
            dve.wait_ge(d_in, 16)
            nc.vector.tensor_scalar(d_clip[:], d_sb[:], 0.0, 1.0, ALU.max, ALU.min).then_inc(d_set, 1)
            dve.wait_ge(wT_done, 1)
            nc.vector.tensor_copy(wT[:], psS[:, 0:P]).then_inc(wT_set, 1)
            dve.wait_ge(d_set, 1)
            nc.vector.tensor_scalar(wTd[:], psS[:, 0:P], d_clip[:, 0:1], DT, ALU.mult, ALU.mult).then_inc(wTd_set, 1)
            nc.vector.memset(u_split[:].bitcast(F32), 0.0).then_inc(u_chain, 1)
            dve.wait_ge(gate_set, 1)
            dve.wait_ge(ident_set, 1)
            for t in range(T):
                dve.wait_ge(adj_in[t], 16)
                nc.vector.tensor_scalar(L[:, t], adj_sb[:, t, :].rearrange("p (q c) -> p c q", c=T), gate[:, t:t + 1],
                                        None, ALU.mult).then_inc(L_scaled, 1)
                dve.wait_ge(L_scaled, t + 1)
                nc.vector.scalar_tensor_tensor(L[:, t, t, :], ident[:], diag[:, t:t + 1], L[:, t, t, :], ALU.mult,
                                               ALU.add).then_inc(L_set, 1)
            statistics(0, 0, 0)
            normalize(0, 0)
            statistics(1, 1, 0)
            for t in range(T):
                power_lo(LT_hi_set, LT_hi, LT_lo, LT_lo_set, t)
            x0_lo(0, 0)
            nc.vector.memset(u_col[:], 1.0).then_inc(u_chain, 1)
            dve.wait_ge(u_chain, 2)
            dve.wait_ge(L_set, T)
            nc.vector.tensor_reduce(u_col[:, :, 1], L[:].rearrange("p t c q -> p t (c q)"), AX.X, ALU.add).then_inc(u_chain, 1)
            normalize(1, 1)
            statistics(2, 2, 0)
            for t in range(T):
                power_lo(L2T_hi_set, L2T_hi, L2T_lo, L2T_lo_set, t)
            split_u(3)
            xT_lo(0, 0)
            z_lo(0, 0, 1)
            x0_lo(1, 1)
            for t in range(T):
                power_lo(L3T_hi_set, L3T_hi, L3T_lo, L3T_lo_set, t)
                if t == 0:
                    dve.wait_ge(FR_set, 3)
                    dve.wait_ge(dt_ident_set, 1)
                    for i in range(STEPS):
                        if i:
                            dve.wait_ge(C_sum, i)
                        for k in range(STEPS - i):
                            s, c = place[k]
                            block_k = C[:, s, c * P:(c + 1) * P]
                            ins = nc.vector.scalar_tensor_tensor(block_k, R[:, i, :] if i else dt_ident[:],
                                                                 DT * comb(k + i, k) if i else 1.0, block_k,
                                                                 ALU.mult, ALU.add)
                        ins.then_inc(C_sum, 1)
                if t == 1:
                    dve.wait_ge(g_done, 1)
                    dve.wait_ge(b_in, 16)
                    for k in range(STEPS + 1):
                        col = psS[:, 8 - k:9 - k] if k < 8 else b_sb[:]
                        for o in (0, 3):
                            ins = nc.vector.tensor_scalar(g_col[:, k // 3, k % 3 + o:k % 3 + o + 1], col,
                                                          float(comb(8, k)), None, ALU.mult)
                    ins.then_inc(g_set, 1)
                if t == 2:
                    dve.wait_ge(g_rows_done, 1)
                    nc.vector.tensor_copy(g_rows[:], psS[0:6, 0:3 * P]).then_inc(g_rows_set, 1)
            normalize(2, 0)
            statistics(3, 3, 0)
            keep_u_rows(0, 1)
            z_lo(0, 0, 2)
            x0_lo(2, 0)
            dve.wait_ge(u_cols_done, 1)
            nc.vector.tensor_copy(u_col[:, :, 2], psS[:, 0:4 * T].rearrange("p (t u) -> p t u", u=4)[:, :, 1]).then_inc(u_chain, 1)
            split_u(5)
            xT_lo(1, 1)
            dve.wait_ge(C_hi_set, 1)
            lo_part(C_lo[:], C[:], C_hi[:]).then_inc(C_lo_set, 1)
            z_lo(1, 1, 1)
            keep_u_rows(1, 2)
            z_lo(1, 1, 2)
            keep_u_rows(2, 3)
            dve.wait_ge(u_cols_done, 2)
            nc.vector.tensor_copy(u_col[:], psS[:, 0:4 * T].rearrange("p (t u) -> p t u", u=4)[:, :, 0:3]).then_inc(u_chain, 1)
            split_u(7)
            keep_u_rows(3, 4)
            dve.wait_ge(bias_done, 1)
            nc.vector.tensor_copy(bias[:], psS[:]).then_inc(bias_set, 1)
            normalize(3, 1)
            x0_lo(3, 1)
            with dve.Fori(0, G - 1) as g:
                group(g)
            group(G - 1, last=True)


_INS = ["x", "adj", "L0_gnn_alpha_train", "L0_gnn_w", "L0_gnn_d", "L0_gnn_fc_in_w", "L0_gnn_fc_in_b"]


def kernel(**inputs):
    import numpy as np
    import concourse.bacc as bacc
    from concourse.bass_utils import run_bass_kernel_spmd

    nc = bacc.Bacc("TRN2", target_bir_lowering=False, num_devices=1)
    arrays, args = {}, []
    for name in _INS:
        a = np.ascontiguousarray(inputs[name])
        arrays[f"in_{name}"] = a
        args.append(nc.dram_tensor(f"in_{name}", a.shape, mybir.dt.from_np(a.dtype), kind="ExternalInput").ap())
    args.append(nc.dram_tensor("out_0", arrays["in_x"].shape, F32, kind="ExternalOutput").ap())
    build(nc, *args)
    r = run_bass_kernel_spmd(nc, [arrays], core_ids=[0])
    return r.results[0]["out_0"]
```

```python
from contextlib import ExitStack
from math import comb

import concourse.bass as bass
from concourse import mybir

ALU = mybir.AluOpType
ACT = mybir.ActivationFunctionType
AX = mybir.AxisListType
F32 = mybir.dt.float32
F32R = mybir.dt.float32r

P = 128
STEPS = 8
DT = 1.0 / STEPS
EPS = 1e-5
GB = 4


def build(nc, x, adj, alpha, w, d, fc_w, fc_b, out):
    B, N, D = x.shape
    T = N // P
    G = B // GB
    assert D == P and N == T * P and GB * D == 512 and N == 512 and B == G * GB
    place = {3 * (2 - c) + s: (s, c) for s in range(3) for c in range(3)}

    x_dram = x.rearrange("b (p t) d -> b p (t d)", t=T)
    out_dram = out.rearrange("(g b) (p t) d -> g t p b d", b=GB, t=T)
    adj_dram = adj.rearrange("(p t) m -> t p m", t=T)

    with ExitStack() as ctx:
        def sb(name, shape, dt=F32):
            return ctx.enter_context(nc.sbuf_tensor(name, shape, dt))

        def psum(name, shape):
            return ctx.enter_context(nc.psum_tensor(name, shape, F32))

        def sem(name):
            return ctx.enter_context(nc.semaphore(name))

        def pair(name, shape):
            return sb(name + "_hi", shape, F32R), sb(name + "_lo", shape, F32R)

        xs = sb("xs", [P, B, T, D])
        ident = sb("ident", [P, P])
        dt_ident = sb("dt_ident", [P, P])
        ones, unused = sb("ones", [P, 1]), sb("unused", [P, 2])
        sel = sb("sel", [P, 4])
        adj_sb = sb("adj_sb", [P, T, N])
        alpha_sb = sb("alpha_sb", [P, T])
        exp_alpha = sb("exp_alpha", [P, T])
        gate = sb("gate", [P, T])
        diag = sb("diag", [P, T])
        L = sb("L", [P, T, T, P])
        L_hi, L_lo = pair("L", [P, T, T, P])
        LT_hi, LT_lo = pair("LT", [P, T, N])
        L2T_hi, L2T_lo = pair("L2T", [P, T, N])
        L3T_hi, L3T_lo = pair("L3T", [P, T, N])
        w_sb = sb("w_sb", [P, P])
        d_sb = sb("d_sb", [P, 1])
        d_clip = sb("d_clip", [P, 1])
        wT = sb("wT", [P, P])
        wTd = sb("wTd", [P, P])
        fc_sb = sb("fc_sb", [P, P])
        b_sb = sb("b_sb", [P, 1])
        R = sb("R", [P, STEPS + 1, P])
        C = sb("C", [P, 3, 3 * P])
        C_hi, C_lo = pair("C", [P, 3, 3 * P])
        u_col = sb("u_col", [P, T, 3])
        u_split = sb("u_split", [P, T, P], F32R)
        u_rows = sb("u_rows", [P, N])
        g_col = sb("g_col", [P, P])
        g_rows = sb("g_rows", [P, P])
        bias = sb("bias", [P, T * D])
        stats = sb("stats", [P, T, 6])
        halves, halves_apart, apart_sq = sb("halves", [P, T, 2]), sb("halves_apart", [P, T]), sb("apart_sq", [P, T])
        mean = sb("mean", [P, T])
        var_eps, std, rstd0, newton, rstd = (sb(n, [P, T]) for n in ("var_eps", "std", "rstd0", "newton", "rstd"))
        normed = [sb(f"normed{n}", [P, T, D]) for n in range(2)]
        x0 = [pair(f"x0_{n}", [P, T, D]) for n in range(2)]
        srcT = [[pair(f"src{s}T_{n}", [P, N]) for s in range(3)] for n in range(2)]
        q2_hi, q2_lo = pair("q2", [P, T, GB, D])
        r1 = adj_sb[:].rearrange("p t (b d) -> p t b d", b=GB)
        y1_sum = [sb(f"y1_sum{n}", [P, GB * D]) for n in range(2)]
        y1_hi, y1_lo = (a[:].rearrange("p t c q -> p t (c q)") for a in (L_hi, L_lo))

        psW = psum("psW", [P, T, 512])
        psZ = psum("psZ", [P, 2, 512])
        psT = psum("psT", [P, 512])
        psS = psum("psS", [P, 512])

        adj_in = [sem(f"adj_in{t}") for t in range(T)]
        alpha_in, w_in, d_in, fc_in, b_in = (sem(n) for n in ("alpha_in", "w_in", "d_in", "fc_in", "b_in"))
        x_in = [sem(f"x_in{j}") for j in range(GB)]
        zeros_set, ident_set, sel_set, dt_ident_set = (sem(n) for n in ("zeros_set", "ident_set", "sel_set", "dt_ident_set"))
        ones_set, u_zero = sem("ones_set"), sem("u_zero")
        exp_set, gate_chain, gate_set = sem("exp_set"), sem("gate_chain"), sem("gate_set")
        L_scaled, L_set, L_hi_set, L_lo_set = sem("L_scaled"), sem("L_set"), sem("L_hi_set"), sem("L_lo_set")
        LT_done, LT_hi_set, LT_lo_set = sem("LT_done"), sem("LT_hi_set"), sem("LT_lo_set")
        L2T_done, L2T_hi_set, L2T_lo_set = sem("L2T_done"), sem("L2T_hi_set"), sem("L2T_lo_set")
        L3T_done, L3T_hi_set, L3T_lo_set = sem("L3T_done"), sem("L3T_hi_set"), sem("L3T_lo_set")
        d_set, wT_done, wTd_set = sem("d_set"), sem("wT_done"), sem("wTd_set")
        R_done, R_set = sem("R_done"), sem("R_set")
        FR_done, FR_set, C_sum, C_hi_set, C_lo_set = sem("FR_done"), sem("FR_set"), sem("C_sum"), sem("C_hi_set"), sem("C_lo_set")
        g_done, g_set, g_rows_done, g_rows_set = sem("g_done"), sem("g_set"), sem("g_rows_done"), sem("g_rows_set")
        u_chain, u_split_set, u_rows_done, u_rows_set = sem("u_chain"), sem("u_split_set"), sem("u_rows_done"), sem("u_rows_set")
        u_cols_done, bias_done, bias_set = sem("u_cols_done"), sem("bias_done"), sem("bias_set")
        ln_chain, std_set, normed_set, x0_hi_set, x0_lo_set = sem("ln_chain"), sem("std_set"), sem("normed_set"), sem("x0_hi_set"), sem("x0_lo_set")
        xT_done, xT_hi_set, xT_lo_set = sem("xT_done"), sem("xT_hi_set"), sem("xT_lo_set")
        z_done, z_hi_set, z_lo_set = sem("z_done"), sem("z_hi_set"), sem("z_lo_set")
        c_done, c_hi_set, c_lo_set, bias_added = sem("c_done"), sem("c_hi_set"), sem("c_lo_set"), sem("bias_added")
        y1_done, y1_sum_set, y1_hi_set, y1_lo_set = sem("y1_done"), sem("y1_sum_set"), sem("y1_hi_set"), sem("y1_lo_set")
        y_done, y_set, stored = sem("y_done"), sem("y_set"), sem("stored")

        LN = 9
        LN_VAR = 5

        block = ctx.enter_context(nc.Block())

        @block.sync
        def _(sp):
            sp.dma_start(alpha_sb[:], alpha.rearrange("(p t) -> p t", t=T)).then_inc(alpha_in, 16)
            for t in range(T):
                sp.dma_start(adj_sb[:, t, :], adj_dram[t]).then_inc(adj_in[t], 16)
            for j in range(GB):
                sp.dma_start(xs[:, j, :, :], x_dram[j]).then_inc(x_in[j], 16)
            with sp.Fori(1, G) as g:
                for j in range(GB):
                    sp.wait_ge(x_in[j], 16 * g)
                    sp.dma_start(xs[:, bass.ds(GB * g + j, 1), :, :],
                                 x_dram[bass.ds(GB * g + j, 1)].rearrange("o p n -> (o p) n")).then_inc(x_in[j], 16)
            with sp.Fori(0, G) as g:
                for t in range(T):
                    sp.wait_ge(y_set, T * g + t + 1)
                    sp.dma_start(out_dram[bass.ds(g, 1), t].rearrange("o p b d -> (o p) b d"),
                                 xs[:, bass.ds(GB * g, GB), t, :]).then_inc(stored, 16)
            sp.wait_ge(stored, 16 * G * T)

        @block.gpsimd
        def _(pool):
            nc.gpsimd.memset(ident[:], 0.0).then_inc(zeros_set, 1)
            nc.gpsimd.memset(sel[:], 0.0).then_inc(zeros_set, 1)
            pool.wait_ge(zeros_set, 2)
            nc.gpsimd.affine_select(out=ident[:], in_=ident[:], compare_op=ALU.not_equal, fill=1.0, base=0,
                                    pattern=[[-1, P]], channel_multiplier=1).then_inc(ident_set, 1)
            for o in (0, 3):
                if o:
                    pool.wait_ge(sel_set, 1)
                nc.gpsimd.affine_select(out=sel[:], in_=sel[:], compare_op=ALU.not_equal, fill=1.0, base=-32 - o,
                                        pattern=[[-1, 4]], channel_multiplier=1).then_inc(sel_set, 1)
            pool.wait_ge(ident_set, 1)
            nc.gpsimd.tensor_scalar(dt_ident[:], ident[:], DT, 0.0, ALU.mult, ALU.add).then_inc(dt_ident_set, 1)
            for t in range(T):
                pool.wait_ge(L_hi_set, t + 1)
                nc.gpsimd.tensor_tensor(L_lo[:, t], L[:, t], L_hi[:, t].bitcast(F32), ALU.subtract).then_inc(L_lo_set, 1)

            def group(g):
                for j in range(GB):
                    pool.wait_ge(c_lo_set, 2 * (GB * g + j) + 2)
                    xb = xs[:, bass.ds(GB * g + j, 1), :, :].rearrange("p o t d -> p (o t d)")
                    nc.gpsimd.tensor_tensor(xb, xb, bias[:], ALU.add).then_inc(bias_added, 1)
                for t in range(T):
                    pool.wait_ge(y1_hi_set, T * g + t + 1)
                    nc.gpsimd.tensor_tensor(y1_lo[:, t], y1_sum[t % 2][:], y1_hi[:, t].bitcast(F32),
                                            ALU.subtract).then_inc(y1_lo_set, 1)

            pool.wait_ge(bias_set, 1)
            with pool.Fori(0, G) as g:
                group(g)

        @block.scalar
        def _(act):
            act.dma_start(w_sb[:], w).then_inc(w_in, 16)
            act.dma_start(d_sb[:], d.rearrange("(p o) -> p o", o=1)).then_inc(d_in, 16)
            act.dma_start(fc_sb[:], fc_w).then_inc(fc_in, 16)
            act.dma_start(b_sb[:], fc_b.rearrange("(p o) -> p o", o=1)).then_inc(b_in, 16)
            act.wait_ge(ones_set, 1)
            nc.scalar.activation(unused[:, 0:1], ones[:], ACT.Exp)
            act.wait_ge(alpha_in, 16)
            nc.scalar.activation(exp_alpha[:], alpha_sb[:], ACT.Exp, scale=-1.0).then_inc(exp_set, 1)
            nc.scalar.activation(unused[:, 1:2], ones[:], ACT.Sqrt)

            def power_of_r(n, lo, hi):
                act.wait_ge(R_done, n)
                nc.scalar.activation(R[:, lo:hi, :], psS[:, 0:(hi - lo) * P], ACT.Copy).then_inc(R_set, 1)

            def split_L(t):
                act.wait_ge(L_set, t + 1)
                nc.scalar.activation(L_hi[:, t], L[:, t], ACT.Copy).then_inc(L_hi_set, 1)

            def power_hi(done, count, hi, hi_set, t):
                act.wait_ge(done, count)
                nc.scalar.activation(hi[:, t, :], psW[:, t, :], ACT.Copy).then_inc(hi_set, 1)

            def fr_scaled(n):
                act.wait_ge(FR_done, n + 1)
                for j in range(3 * n, 3 * n + 3):
                    s, c = place[8 - j]
                    ins = nc.scalar.activation(C[:, s, c * P:(c + 1) * P], psS[:, (j - 3 * n) * P:(j - 3 * n + 1) * P],
                                               ACT.Copy, scale=float(comb(8, j)))
                ins.then_inc(FR_set, 1)

            def deviation(i):
                act.wait_ge(ln_chain, LN * i + LN_VAR)
                nc.scalar.activation(std[:], var_eps[:], ACT.Sqrt).then_inc(std_set, 1)

            def x0_hi(i, n):
                act.wait_ge(normed_set, i + 1)
                if not (isinstance(i, int) and i < 2):
                    act.wait_ge(z_done, 2 * i - 2)
                nc.scalar.activation(x0[n][0][:], normed[n][:], ACT.Relu).then_inc(x0_hi_set, 1)

            def xT_hi(i, n):
                act.wait_ge(xT_done, i + 1)
                nc.scalar.activation(srcT[n][0][0][:], psT[:], ACT.Relu).then_inc(xT_hi_set, 1)

            def z_hi(i, n, s):
                act.wait_ge(z_done, 2 * i + s)
                nc.scalar.activation(srcT[n][s][0][:], psZ[:, s - 1, :], ACT.Copy).then_inc(z_hi_set, 1)

            def c_hi(i, j):
                for h in range(2):
                    act.wait_ge(c_done, 2 * i + h + 1)
                    nc.scalar.activation(q2_hi[:, 2 * h:2 * h + 2, j, :], psW[:, 2 * h:2 * h + 2, 0:P], ACT.Copy)
                    nc.scalar.activation(r1[:, 2 * h:2 * h + 2, j, :], psW[:, 2 * h:2 * h + 2, P:2 * P],
                                         ACT.Copy).then_inc(c_hi_set, 1)

            def y1_hi_part(g):
                for t in range(T):
                    act.wait_ge(y1_sum_set, T * g + t + 1)
                    nc.scalar.activation(y1_hi[:, t], y1_sum[t % 2][:], ACT.Copy).then_inc(y1_hi_set, 1)

            def group(g, last=False):
                xT_hi(GB * g + 2, 0)
                z_hi(GB * g + 2, 0, 1)
                z_hi(GB * g + 2, 0, 2)
                c_hi(GB * g + 1, 1)
                xT_hi(GB * g + 3, 1)
                z_hi(GB * g + 3, 1, 1)
                z_hi(GB * g + 3, 1, 2)
                if not last:
                    deviation(GB * g + 4)
                c_hi(GB * g + 2, 2)
                if not last:
                    x0_hi(GB * g + 4, 0)
                    deviation(GB * g + 5)
                c_hi(GB * g + 3, 3)
                if not last:
                    x0_hi(GB * g + 5, 1)
                    deviation(GB * g + 6)
                    xT_hi(GB * g + 4, 0)
                    z_hi(GB * g + 4, 0, 1)
                    z_hi(GB * g + 4, 0, 2)
                    x0_hi(GB * g + 6, 0)
                    deviation(GB * g + 7)
                y1_hi_part(g)
                if not last:
                    xT_hi(GB * g + 5, 1)
                    z_hi(GB * g + 5, 1, 1)
                    z_hi(GB * g + 5, 1, 2)
                    x0_hi(GB * g + 7, 1)
                    c_hi(GB * g + 4, 0)

            split_L(0)
            power_of_r(1, 1, 2)
            split_L(1)
            split_L(2)
            power_of_r(2, 2, 3)
            split_L(3)
            power_of_r(3, 3, 5)
            for t in range(T):
                power_hi(LT_done, 1, LT_hi, LT_hi_set, t)
                if t == 1:
                    power_of_r(4, 5, 9)
            fr_scaled(0)
            deviation(0)
            x0_hi(0, 0)
            for t in range(T):
                power_hi(L2T_done, t + 1, L2T_hi, L2T_hi_set, t)
                if t < 2:
                    fr_scaled(t + 1)
            deviation(1)
            xT_hi(0, 0)
            z_hi(0, 0, 1)
            act.wait_ge(C_sum, STEPS)
            nc.scalar.activation(C_hi[:], C[:], ACT.Copy).then_inc(C_hi_set, 1)
            x0_hi(1, 1)
            for t in range(T):
                power_hi(L3T_done, t + 1, L3T_hi, L3T_hi_set, t)
            deviation(2)
            z_hi(0, 0, 2)
            x0_hi(2, 0)
            xT_hi(1, 1)
            z_hi(1, 1, 1)
            z_hi(1, 1, 2)
            deviation(3)
            x0_hi(3, 1)
            c_hi(0, 0)
            with act.Fori(0, G - 1) as g:
                group(g)
            group(G - 1, last=True)

        @block.tensor
        def _(pe):
            def product(o, a, b, start, stop):
                nc.tensor.matmul(o, a[0], b[0], start=start, stop=False)
                nc.tensor.matmul(o, a[0], b[1], start=False, stop=False)
                return nc.tensor.matmul(o, a[1], b[0], start=False, stop=stop)

            def power_tile(b_hi, b_lo, t):
                for k in range(T):
                    ins = product(psW[:, t, :], (L_hi[:, k, t, :], L_lo[:, k, t, :]), (b_hi[:, k, :], b_lo[:, k, :]),
                                  k == 0, k == T - 1)
                return ins

            def transpose_x(i, n):
                pe.wait_ge(normed_set, i + 1)
                if not (isinstance(i, int) and i < 1):
                    pe.wait_ge(xT_lo_set, i)
                for t in range(T):
                    ins = nc.tensor.transpose(psT[:, t * P:(t + 1) * P], normed[n][:, t, :], ident[:])
                ins.then_inc(xT_done, 1)

            def make_z(i, n, s):
                if s == 1:
                    pe.wait_ge(x0_lo_set, i + 1)
                if not (isinstance(i, int) and i < 1):
                    pe.wait_ge(z_lo_set, 2 * i - 2 + s)
                lsT_hi, lsT_lo = (LT_hi, LT_lo) if s == 1 else (L2T_hi, L2T_lo)
                for m in range(T):
                    ins = product(psZ[:, s - 1, :], (x0[n][0][:, m, :], x0[n][1][:, m, :]),
                                  (lsT_hi[:, m, :], lsT_lo[:, m, :]), m == 0, m == T - 1)
                ins.then_inc(z_done, 1)

            def make_c(i, j, n):
                pe.wait_ge(xT_lo_set, i + 1)
                pe.wait_ge(z_lo_set, 2 * i + 2)
                for t in range(T):
                    if t % 2 == 0 and j > 0:
                        pe.wait_ge(c_lo_set, 2 * i - 1 + t // 2)
                    nodes = slice(t * P, (t + 1) * P)
                    for s in range(3):
                        ins = product(psW[:, t, 0:3 * P], (srcT[n][s][0][:, nodes], srcT[n][s][1][:, nodes]),
                                      (C_hi[:, s, :], C_lo[:, s, :]), s == 0, s == 2)
                    if t % 2 == 1:
                        ins.then_inc(c_done, 1)

            def make_y1(g):
                for t in range(T):
                    nodes = slice(t * P, (t + 1) * P)
                    for m in range(T):
                        if t == 0 and m % 2 == 0:
                            pe.wait_ge(c_lo_set, 2 * GB * g + 2 * GB - 1 + m // 2)
                        ins = product(psW[:, t, :], (L3T_hi[:, m, nodes], L3T_lo[:, m, nodes]),
                                      (q2_hi[:, m], q2_lo[:, m]), m == 0, m == T - 1)
                    ins.then_inc(y1_done, 1)

            def make_y(g):
                for t in range(T):
                    nodes = slice(t * P, (t + 1) * P)
                    for m in range(T):
                        if t == 0:
                            pe.wait_ge(y1_lo_set, T * g + m + 1)
                        ins = product(psW[:, t, :], (L3T_hi[:, m, nodes], L3T_lo[:, m, nodes]),
                                      (y1_hi[:, m], y1_lo[:, m]), m == 0, m == T - 1)
                    ins.then_inc(y_done, 1)

            def group(g, last=False):
                transpose_x(GB * g + 2, 0)
                make_z(GB * g + 2, 0, 1)
                make_z(GB * g + 2, 0, 2)
                make_c(GB * g + 1, 1, 1)
                transpose_x(GB * g + 3, 1)
                make_z(GB * g + 3, 1, 1)
                make_z(GB * g + 3, 1, 2)
                make_c(GB * g + 2, 2, 0)
                make_c(GB * g + 3, 3, 1)
                if not last:
                    transpose_x(GB * g + 4, 0)
                    make_z(GB * g + 4, 0, 1)
                    make_z(GB * g + 4, 0, 2)
                make_y1(g)
                if not last:
                    transpose_x(GB * g + 5, 1)
                    make_z(GB * g + 5, 1, 1)
                    make_z(GB * g + 5, 1, 2)
                make_y(g)
                if not last:
                    pe.wait_ge(y_set, T * g + T)
                    make_c(GB * g + 4, 0, 0)

            def u_times(b_hi, b_lo):
                for n, (b, m) in enumerate([(b, m) for b in (b_hi, b_lo) for m in range(T)]):
                    ins = nc.tensor.matmul(psS[:], u_split[:, m, :], b[:, m, :], start=(n == 0), stop=(n == 2 * T - 1))
                ins.then_inc(u_rows_done, 1)

            def u_columns():
                for t in range(T):
                    ins = nc.tensor.matmul(psS[:, 4 * t:4 * t + 4], u_rows[:, t * P:(t + 1) * P], sel[:],
                                           start=True, stop=True)
                ins.then_inc(u_cols_done, 1)

            def power_of_r(n, by, lo, hi):
                pe.wait_ge(R_set, n)
                nc.tensor.matmul(psS[:, 0:(hi - lo) * P], R[:, by, :], R[:, lo:hi, :], start=True,
                                 stop=True).then_inc(R_done, 1)

            def transpose_l(t):
                pe.wait_ge(L_set, t + 1)
                for m in range(T):
                    ins = nc.tensor.transpose(psW[:, m, t * P:(t + 1) * P], L[:, t, m, :], ident[:])
                if t == T - 1:
                    ins.then_inc(LT_done, 1)

            pe.wait_ge(ident_set, 1)
            pe.wait_ge(w_in, 16)
            nc.tensor.transpose(psS[:, 0:P], w_sb[:], ident[:]).then_inc(wT_done, 1)
            transpose_l(0)
            pe.wait_ge(wTd_set, 1)
            nc.tensor.matmul(psS[:, 0:P], wTd[:], wT[:], start=True, stop=True).then_inc(R_done, 1)
            transpose_l(1)
            transpose_l(2)
            power_of_r(1, 1, 1, 2)
            transpose_l(3)
            power_of_r(2, 2, 1, 3)
            power_of_r(3, 4, 1, 5)
            pe.wait_ge(fc_in, 16)
            pe.wait_ge(R_set, 4)
            nc.tensor.matmul(psS[:, 0:P], fc_sb[:], ident[:], start=True, stop=True)
            nc.tensor.matmul(psS[:, P:3 * P], fc_sb[:], R[:, 1:3, :], start=True, stop=True).then_inc(FR_done, 1)
            pe.wait_ge(L_lo_set, T)
            pe.wait_ge(LT_lo_set, T)
            for t in range(T):
                power_tile(LT_hi, LT_lo, t).then_inc(L2T_done, 1)
                if t < 2:
                    pe.wait_ge(FR_set, t + 1)
                    nc.tensor.matmul(psS[:, 0:3 * P], fc_sb[:], R[:, 3 * t + 3:3 * t + 6, :], start=True,
                                     stop=True).then_inc(FR_done, 1)
            transpose_x(0, 0)
            make_z(0, 0, 1)
            pe.wait_ge(FR_set, 3)
            pe.wait_ge(b_in, 16)
            for j in range(1, STEPS + 1):
                ins = nc.tensor.matmul(psS[:, j:j + 1], R[:, j, :], b_sb[:], start=True, stop=True)
            ins.then_inc(g_done, 1)
            pe.wait_ge(L2T_lo_set, T)
            power_tile(L2T_hi, L2T_lo, 0).then_inc(L3T_done, 1)
            pe.wait_ge(g_set, 1)
            pe.wait_ge(u_split_set, 1)
            u_times(LT_hi, LT_lo)
            power_tile(L2T_hi, L2T_lo, 1).then_inc(L3T_done, 1)
            pe.wait_ge(u_rows_set, 1)
            nc.tensor.transpose(psS[:, 0:P], g_col[:], ident[:]).then_inc(g_rows_done, 1)
            power_tile(L2T_hi, L2T_lo, 2).then_inc(L3T_done, 1)
            pe.wait_ge(g_rows_set, 1)
            pe.wait_ge(sel_set, 2)
            u_columns()
            power_tile(L2T_hi, L2T_lo, 3).then_inc(L3T_done, 1)
            pe.wait_ge(u_split_set, 2)
            for t in range(T):
                ins = nc.tensor.transpose(psS[:, t * P:(t + 1) * P], u_split[:, t, :].bitcast(F32), ident[:])
            ins.then_inc(u_rows_done, 1)
            make_z(0, 0, 2)
            pe.wait_ge(u_rows_set, 2)
            pe.wait_ge(L3T_lo_set, T)
            u_times(L3T_hi, L3T_lo)
            transpose_x(1, 1)
            make_z(1, 1, 1)
            pe.wait_ge(u_rows_set, 3)
            u_columns()
            make_z(1, 1, 2)
            pe.wait_ge(u_split_set, 3)
            u_times(L3T_hi, L3T_lo)
            pe.wait_ge(C_lo_set, 1)
            make_c(0, 0, 0)
            pe.wait_ge(u_rows_set, 4)
            for t in range(T):
                ins = nc.tensor.matmul(psS[:, t * P:(t + 1) * P], u_rows[:, t * P:(t + 1) * P], g_rows[:],
                                       start=True, stop=True)
            ins.then_inc(bias_done, 1)
            with pe.Fori(0, G - 1) as g:
                group(g)
            group(G - 1, last=True)

        @block.vector
        def _(dve):
            def lo_part(lo, full, hi):
                return nc.vector.tensor_tensor(lo, full, hi.bitcast(F32), ALU.subtract)

            def power_lo(hi_set, hi, lo, lo_set, t):
                dve.wait_ge(hi_set, t + 1)
                lo_part(lo[:, t, :], psW[:, t, :], hi[:, t, :]).then_inc(lo_set, 1)

            def statistics(i, j, g):
                dve.wait_ge(x_in[j], 16 * g + 16)
                xb = xs[:, bass.ds(i, 1), :, :]
                for t in range(T):
                    ins = nc.vector.bn_stats(stats[:, t, :], xb[:, :, t, :].rearrange("p o d -> p (o d)"))
                ins.then_inc(ln_chain, 1)
                dve.wait_ge(ln_chain, LN * i + 1)
                nc.vector.tensor_tensor(halves[:], stats[:, :, 1:3], stats[:, :, 4:6], ALU.add)
                nc.vector.tensor_tensor(halves_apart[:], stats[:, :, 1], stats[:, :, 4],
                                        ALU.subtract).then_inc(ln_chain, 1)
                dve.wait_ge(ln_chain, LN * i + 2)
                nc.vector.tensor_scalar(mean[:], halves[:, :, 0], 0.5, None, ALU.mult)
                nc.vector.tensor_tensor(apart_sq[:], halves_apart[:], halves_apart[:], ALU.mult).then_inc(ln_chain, 1)
                dve.wait_ge(ln_chain, LN * i + 3)
                nc.vector.scalar_tensor_tensor(apart_sq[:], apart_sq[:], D / 4.0, halves[:, :, 1], ALU.mult,
                                               ALU.add).then_inc(ln_chain, 1)
                dve.wait_ge(ln_chain, LN * i + 4)
                nc.vector.tensor_scalar(var_eps[:], apart_sq[:], 1.0 / D, EPS, ALU.mult, ALU.add).then_inc(ln_chain, 1)

            def normalize(i, n):
                dve.wait_ge(std_set, i + 1)
                nc.vector.reciprocal(rstd0[:], std[:]).then_inc(ln_chain, 1)
                dve.wait_ge(ln_chain, LN * i + 6)
                nc.vector.tensor_tensor(newton[:], var_eps[:], rstd0[:], ALU.mult).then_inc(ln_chain, 1)
                dve.wait_ge(ln_chain, LN * i + 7)
                nc.vector.scalar_tensor_tensor(newton[:], newton[:], -0.5, rstd0[:], ALU.mult, ALU.mult).then_inc(ln_chain, 1)
                dve.wait_ge(ln_chain, LN * i + 8)
                nc.vector.scalar_tensor_tensor(rstd[:], newton[:], 1.5, rstd0[:], ALU.add, ALU.mult).then_inc(ln_chain, 1)
                dve.wait_ge(ln_chain, LN * i + 9)
                xb = xs[:, bass.ds(i, 1), :, :]
                if not (isinstance(i, int) and i < 2):
                    dve.wait_ge(xT_done, i - 1)
                    dve.wait_ge(x0_hi_set, i - 1)
                for t in range(T):
                    ins = nc.vector.tensor_scalar(normed[n][:, t, :], xb[:, :, t, :].rearrange("p o d -> p (o d)"),
                                                  mean[:, t:t + 1], rstd[:, t:t + 1], ALU.subtract, ALU.mult)
                ins.then_inc(normed_set, 1)

            def relu_lo(lo, full, hi):
                return nc.vector.scalar_tensor_tensor(lo, full, 0.0, hi.bitcast(F32), ALU.max, ALU.subtract)

            def x0_lo(i, n):
                dve.wait_ge(x0_hi_set, i + 1)
                relu_lo(x0[n][1][:], normed[n][:], x0[n][0][:]).then_inc(x0_lo_set, 1)

            def xT_lo(i, n):
                dve.wait_ge(xT_hi_set, i + 1)
                relu_lo(srcT[n][0][1][:], psT[:], srcT[n][0][0][:]).then_inc(xT_lo_set, 1)

            def z_lo(i, n, s):
                dve.wait_ge(z_hi_set, 2 * i + s)
                lo_part(srcT[n][s][1][:], psZ[:, s - 1, :], srcT[n][s][0][:]).then_inc(z_lo_set, 1)

            def c_lo(i, j):
                for h in range(2):
                    dve.wait_ge(c_hi_set, 2 * i + h + 1)
                    t2 = slice(2 * h, 2 * h + 2)
                    lo_part(q2_lo[:, t2, j, :], psW[:, t2, 0:P], q2_hi[:, t2, j, :])
                    xb = xs[:, bass.ds(i, 1), t2, :].rearrange("p o t d -> p (o t) d")
                    nc.vector.tensor_tensor(xb, psW[:, t2, 2 * P:3 * P], xb, ALU.add).then_inc(c_lo_set, 1)

            def y1_part(g):
                for t in range(T):
                    dve.wait_ge(y1_done, T * g + t + 1)
                    if t >= 2:
                        dve.wait_ge(y1_lo_set, T * g + t - 1)
                    nc.vector.tensor_tensor(y1_sum[t % 2][:], psW[:, t, :], r1[:, t].rearrange("p b d -> p (b d)"),
                                            ALU.add).then_inc(y1_sum_set, 1)

            def y_part(g):
                dve.wait_ge(bias_added, GB * g + GB)
                for t in range(T):
                    dve.wait_ge(y_done, T * g + t + 1)
                    xg = xs[:, bass.ds(GB * g, GB), t, :]
                    nc.vector.tensor_tensor(xg, psW[:, t, :].rearrange("p (b d) -> p b d", b=GB), xg,
                                            ALU.add).then_inc(y_set, 1)

            def group(g, last=False):
                xT_lo(GB * g + 2, 0)
                z_lo(GB * g + 2, 0, 1)
                z_lo(GB * g + 2, 0, 2)
                c_lo(GB * g + 1, 1)
                xT_lo(GB * g + 3, 1)
                z_lo(GB * g + 3, 1, 1)
                z_lo(GB * g + 3, 1, 2)
                if not last:
                    statistics(GB * g + 4, 0, g + 1)
                c_lo(GB * g + 2, 2)
                if not last:
                    normalize(GB * g + 4, 0)
                    statistics(GB * g + 5, 1, g + 1)
                    x0_lo(GB * g + 4, 0)
                c_lo(GB * g + 3, 3)
                if not last:
                    normalize(GB * g + 5, 1)
                    statistics(GB * g + 6, 2, g + 1)
                    x0_lo(GB * g + 5, 1)
                    xT_lo(GB * g + 4, 0)
                    z_lo(GB * g + 4, 0, 1)
                    z_lo(GB * g + 4, 0, 2)
                    normalize(GB * g + 6, 0)
                    statistics(GB * g + 7, 3, g + 1)
                    x0_lo(GB * g + 6, 0)
                y1_part(g)
                if not last:
                    xT_lo(GB * g + 5, 1)
                    z_lo(GB * g + 5, 1, 1)
                    z_lo(GB * g + 5, 1, 2)
                    normalize(GB * g + 7, 1)
                    x0_lo(GB * g + 7, 1)
                y_part(g)
                if not last:
                    c_lo(GB * g + 4, 0)

            def split_u(n, block_u):
                dve.wait_ge(u_chain, n)
                o = 32 * block_u
                nc.vector.tensor_copy(u_split[:, :, o:o + 3], u_col[:]).then_inc(u_chain, 1)
                dve.wait_ge(u_chain, n + 1)
                lo_part(u_split[:, :, o + 3:o + 6], u_col[:], u_split[:, :, o:o + 3]).then_inc(u_split_set, 1)

            def keep_u_rows(done, block_to, block_from):
                dve.wait_ge(u_rows_done, done)
                to, fr = 32 * block_to, 32 * block_from
                nc.vector.tensor_copy(u_rows[to:to + 6, :], psS[fr:fr + 6, :]).then_inc(u_rows_set, 1)

            def make_l(t):
                dve.wait_ge(adj_in[t], 16)
                nc.vector.tensor_scalar(L[:, t], adj_sb[:, t, :].rearrange("p (q c) -> p c q", c=T), gate[:, t:t + 1],
                                        None, ALU.mult).then_inc(L_scaled, 1)
                dve.wait_ge(L_scaled, t + 1)
                nc.vector.scalar_tensor_tensor(L[:, t, t, :], ident[:], diag[:, t:t + 1], L[:, t, t, :], ALU.mult,
                                               ALU.add).then_inc(L_set, 1)

            def polynomial(i):
                if i:
                    dve.wait_ge(C_sum, i)
                for k in range(STEPS - i):
                    s, c = place[k]
                    block_k = C[:, s, c * P:(c + 1) * P]
                    ins = nc.vector.scalar_tensor_tensor(block_k, R[:, i, :] if i else dt_ident[:],
                                                         DT * comb(k + i, k) if i else 1.0, block_k,
                                                         ALU.mult, ALU.add)
                ins.then_inc(C_sum, 1)

            nc.vector.memset(ones[:], 1.0).then_inc(ones_set, 1)
            nc.vector.memset(u_split[:].bitcast(F32), 0.0).then_inc(u_zero, 1)
            nc.vector.memset(u_rows[:], 0.0).then_inc(u_zero, 1)
            nc.vector.memset(g_col[:], 0.0).then_inc(u_zero, 1)
            nc.vector.memset(u_col[:], 1.0).then_inc(u_chain, 1)
            dve.wait_ge(exp_set, 1)
            nc.vector.tensor_scalar(exp_alpha[:], exp_alpha[:], 1.0, None, ALU.add).then_inc(gate_chain, 1)
            dve.wait_ge(gate_chain, 1)
            nc.vector.reciprocal(gate[:], exp_alpha[:]).then_inc(gate_chain, 1)
            dve.wait_ge(gate_chain, 2)
            nc.vector.tensor_scalar(gate[:], gate[:], DT * 0.5, None, ALU.mult).then_inc(gate_chain, 1)
            dve.wait_ge(gate_chain, 3)
            nc.vector.tensor_scalar(diag[:], gate[:], -1.0, 1.0 - DT, ALU.mult, ALU.add).then_inc(gate_set, 1)
            dve.wait_ge(gate_set, 1)
            dve.wait_ge(ident_set, 1)
            make_l(0)
            dve.wait_ge(d_in, 16)
            nc.vector.tensor_scalar(d_clip[:], d_sb[:], 0.0, 1.0, ALU.max, ALU.min).then_inc(d_set, 1)
            dve.wait_ge(wT_done, 1)
            nc.vector.tensor_copy(wT[:], psS[:, 0:P])
            dve.wait_ge(d_set, 1)
            nc.vector.tensor_scalar(wTd[:], psS[:, 0:P], d_clip[:, 0:1], DT, ALU.mult, ALU.mult).then_inc(wTd_set, 1)
            for t in range(1, T):
                make_l(t)
            statistics(0, 0, 0)
            for t in range(T):
                power_lo(LT_hi_set, LT_hi, LT_lo, LT_lo_set, t)
            normalize(0, 0)
            statistics(1, 1, 0)
            x0_lo(0, 0)
            dve.wait_ge(u_chain, 1)
            nc.vector.tensor_reduce(u_col[:, :, 1], L[:].rearrange("p t c q -> p t (c q)"), AX.X,
                                    ALU.add).then_inc(u_chain, 1)
            dve.wait_ge(u_zero, 3)
            split_u(2, 1)
            power_lo(L2T_hi_set, L2T_hi, L2T_lo, L2T_lo_set, 0)
            power_lo(L2T_hi_set, L2T_hi, L2T_lo, L2T_lo_set, 1)
            dve.wait_ge(FR_set, 3)
            dve.wait_ge(dt_ident_set, 1)
            polynomial(0)
            power_lo(L2T_hi_set, L2T_hi, L2T_lo, L2T_lo_set, 2)
            polynomial(1)
            power_lo(L2T_hi_set, L2T_hi, L2T_lo, L2T_lo_set, 3)
            for i in range(2, STEPS):
                polynomial(i)
            normalize(1, 1)
            statistics(2, 2, 0)
            dve.wait_ge(g_done, 1)
            dve.wait_ge(b_in, 16)
            for k in range(STEPS + 1):
                col = psS[:, STEPS - k:STEPS + 1 - k] if k < STEPS else b_sb[:]
                for o in (0, 3):
                    at = 32 * (k // 3) + k % 3 + o
                    ins = nc.vector.tensor_scalar(g_col[:, at:at + 1], col, float(comb(STEPS, k)), None, ALU.mult)
            ins.then_inc(g_set, 1)
            xT_lo(0, 0)
            z_lo(0, 0, 1)
            x0_lo(1, 1)
            power_lo(L3T_hi_set, L3T_hi, L3T_lo, L3T_lo_set, 0)
            dve.wait_ge(C_hi_set, 1)
            lo_part(C_lo[:], C[:], C_hi[:]).then_inc(C_lo_set, 1)
            keep_u_rows(1, 1, 1)
            power_lo(L3T_hi_set, L3T_hi, L3T_lo, L3T_lo_set, 1)
            dve.wait_ge(g_rows_done, 1)
            nc.vector.tensor_copy(g_rows[:], psS[:, 0:P]).then_inc(g_rows_set, 1)
            power_lo(L3T_hi_set, L3T_hi, L3T_lo, L3T_lo_set, 2)
            columns = psS[:, 0:4 * T].rearrange("p (t u) -> p t u", u=4)
            dve.wait_ge(u_cols_done, 1)
            nc.vector.tensor_copy(u_col[:, :, 2], columns[:, :, 1]).then_inc(u_chain, 1)
            split_u(4, 1)
            power_lo(L3T_hi_set, L3T_hi, L3T_lo, L3T_lo_set, 3)
            keep_u_rows(2, 0, 1)
            normalize(2, 0)
            statistics(3, 3, 0)
            z_lo(0, 0, 2)
            x0_lo(2, 0)
            keep_u_rows(3, 1, 1)
            xT_lo(1, 1)
            z_lo(1, 1, 1)
            dve.wait_ge(u_cols_done, 2)
            nc.vector.tensor_copy(u_col[:], columns[:, :, 0:3]).then_inc(u_chain, 1)
            split_u(6, 2)
            z_lo(1, 1, 2)
            keep_u_rows(4, 2, 2)
            normalize(3, 1)
            x0_lo(3, 1)
            c_lo(0, 0)
            dve.wait_ge(bias_done, 1)
            nc.vector.tensor_copy(bias[:], psS[:]).then_inc(bias_set, 1)
            with dve.Fori(0, G - 1) as g:
                group(g)
            group(G - 1, last=True)


_INS = ["x", "adj", "L0_gnn_alpha_train", "L0_gnn_w", "L0_gnn_d", "L0_gnn_fc_in_w", "L0_gnn_fc_in_b"]


def kernel(**inputs):
    import numpy as np
    import concourse.bacc as bacc
    from concourse.bass_utils import run_bass_kernel_spmd

    nc = bacc.Bacc("TRN2", target_bir_lowering=False, num_devices=1)
    arrays, args = {}, []
    for name in _INS:
        a = np.ascontiguousarray(inputs[name])
        arrays[f"in_{name}"] = a
        args.append(nc.dram_tensor(f"in_{name}", a.shape, mybir.dt.from_np(a.dtype), kind="ExternalInput").ap())
    args.append(nc.dram_tensor("out_0", arrays["in_x"].shape, F32, kind="ExternalOutput").ap())
    build(nc, *args)
    r = run_bass_kernel_spmd(nc, [arrays], core_ids=[0])
    return r.results[0]["out_0"]
```

```python
from contextlib import ExitStack
from math import comb

import concourse.bass as bass
from concourse import mybir

ALU = mybir.AluOpType
ACT = mybir.ActivationFunctionType
AX = mybir.AxisListType
F32 = mybir.dt.float32
F32R = mybir.dt.float32r

P = 128
STEPS = 8
DT = 1.0 / STEPS
EPS = 1e-5
GB = 4


def build(nc, x, adj, alpha, w, d, fc_w, fc_b, out):
    B, N, D = x.shape
    T = N // P
    G = B // GB
    assert D == P and N == T * P and GB * D == 512 and N == 512 and B == G * GB
    place = {3 * (2 - c) + s: (s, c) for s in range(3) for c in range(3)}

    x_dram = x.rearrange("b (p t) d -> b p (t d)", t=T)
    out_dram = out.rearrange("(g b) (p t) d -> g t p b d", b=GB, t=T)
    adj_dram = adj.rearrange("(p t) m -> t p m", t=T)

    with ExitStack() as ctx:
        def sb(name, shape, dt=F32):
            return ctx.enter_context(nc.sbuf_tensor(name, shape, dt))

        def psum(name, shape):
            return ctx.enter_context(nc.psum_tensor(name, shape, F32))

        def sem(name):
            return ctx.enter_context(nc.semaphore(name))

        def pair(name, shape):
            return sb(name + "_hi", shape, F32R), sb(name + "_lo", shape, F32R)

        xs = sb("xs", [P, B, T, D])
        ident = sb("ident", [P, P])
        ones, unused = sb("ones", [P, 1]), sb("unused", [P, 2])
        binom = sb("binom", [P, STEPS + 1])
        adj_sb = sb("adj_sb", [P, T, N])
        alpha_sb = sb("alpha_sb", [P, T])
        exp_alpha = sb("exp_alpha", [P, T])
        gate = sb("gate", [P, T])
        diag = sb("diag", [P, T])
        L = sb("L", [P, T, T, P])
        L_hi, L_lo = pair("L", [P, T, T, P])
        LT_hi, LT_lo = pair("LT", [P, T, N])
        L2T_hi, L2T_lo = pair("L2T", [P, T, N])
        L3T_hi, L3T_lo = pair("L3T", [P, T, N])
        w_sb = sb("w_sb", [P, P])
        d_sb = sb("d_sb", [P, 1])
        d_clip = sb("d_clip", [P, 1])
        wT = sb("wT", [P, P])
        wTd = sb("wTd", [P, P])
        fc_sb = sb("fc_sb", [P, P])
        b_rows = sb("b_rows", [P, P])
        R = sb("R", [P, STEPS + 1, P])
        C = sb("C", [P, 3, 3 * P])
        C_hi, C_lo = pair("C", [P, 3, 3 * P])
        u_col = sb("u_col", [P, T, 3])
        u_split = sb("u_split", [P, T, P], F32R)
        u_rows = sb("u_rows", [P, N])
        g_raw = sb("g_raw", [P, STEPS + 1])
        g_col = sb("g_col", [P, P])
        g_rows = sb("g_rows", [P, P])
        bias = sb("bias", [P, T * D])
        stats = sb("stats", [P, T, 6])
        halves, halves_apart, apart_sq = sb("halves", [P, T, 2]), sb("halves_apart", [P, T]), sb("apart_sq", [P, T])
        mean = sb("mean", [P, T])
        var_eps, std, rstd0, newton, rstd = (sb(n, [P, T]) for n in ("var_eps", "std", "rstd0", "newton", "rstd"))
        normed = [sb(f"normed{n}", [P, T, D]) for n in range(2)]
        x0 = [pair(f"x0_{n}", [P, T, D]) for n in range(2)]
        srcT = [[pair(f"src{s}T_{n}", [P, N]) for s in range(3)] for n in range(2)]
        q2_hi, q2_lo = pair("q2", [P, T, GB, D])
        g_terms = adj_sb[:].rearrange("p t n -> p (t n)")[:, 0:(STEPS + 1) * P].rearrange("p (k n) -> p k n", n=P)
        r1 = adj_sb[:].rearrange("p t (b d) -> p t b d", b=GB)
        y1_sum = [sb(f"y1_sum{n}", [P, GB * D]) for n in range(2)]
        y1_hi, y1_lo = (a[:].rearrange("p t c q -> p t (c q)") for a in (L_hi, L_lo))

        psW = psum("psW", [P, T, 512])
        psZ = psum("psZ", [P, 2, 512])
        psT = psum("psT", [P, 512])
        psS = psum("psS", [P, 512])

        adj_in = [sem(f"adj_in{t}") for t in range(T)]
        alpha_in, w_in, d_in, fc_in, b_in = (sem(n) for n in ("alpha_in", "w_in", "d_in", "fc_in", "b_in"))
        x_in = [sem(f"x_in{j}") for j in range(GB)]
        zeros_set, ident_set, r0_set, binom_set = (sem(n) for n in ("zeros_set", "ident_set", "r0_set", "binom_set"))
        ones_set, u_zero = sem("ones_set"), sem("u_zero")
        exp_set, gate_chain, gate_set = sem("exp_set"), sem("gate_chain"), sem("gate_set")
        L_scaled, L_set, L_hi_set, L_lo_set = sem("L_scaled"), sem("L_set"), sem("L_hi_set"), sem("L_lo_set")
        LT_done, LT_hi_set, LT_lo_set = sem("LT_done"), sem("LT_hi_set"), sem("LT_lo_set")
        L2T_done, L2T_hi_set, L2T_lo_set = sem("L2T_done"), sem("L2T_hi_set"), sem("L2T_lo_set")
        L3T_done, L3T_hi_set, L3T_lo_set = sem("L3T_done"), sem("L3T_hi_set"), sem("L3T_lo_set")
        d_set, wT_done, wTd_set = sem("d_set"), sem("wT_done"), sem("wTd_set")
        R_done, R_set = sem("R_done"), sem("R_set")
        FR_done, FR_set, C_sum, C_hi_set, C_lo_set = sem("FR_done"), sem("FR_set"), sem("C_sum"), sem("C_hi_set"), sem("C_lo_set")
        g_terms_set, g_raw_set, g_set, g_rows_done, g_rows_set = sem("g_terms_set"), sem("g_raw_set"), sem("g_set"), sem("g_rows_done"), sem("g_rows_set")
        u_chain, u_split_set, u_rows_done, u_rows_set = sem("u_chain"), sem("u_split_set"), sem("u_rows_done"), sem("u_rows_set")
        u_cols_done, bias_done, bias_set = sem("u_cols_done"), sem("bias_done"), sem("bias_set")
        ln_chain, std_set, normed_set, x0_hi_set, x0_lo_set = sem("ln_chain"), sem("std_set"), sem("normed_set"), sem("x0_hi_set"), sem("x0_lo_set")
        xT_done, xT_hi_set, xT_lo_set = sem("xT_done"), sem("xT_hi_set"), sem("xT_lo_set")
        z_done, z_hi_set, z_lo_set = sem("z_done"), sem("z_hi_set"), sem("z_lo_set")
        c_done, q2_lo_set, c_hi_set, c_lo_set, bias_added = sem("c_done"), sem("q2_lo_set"), sem("c_hi_set"), sem("c_lo_set"), sem("bias_added")
        y1_done, y1_sum_set, y1_hi_set, y1_lo_set = sem("y1_done"), sem("y1_sum_set"), sem("y1_hi_set"), sem("y1_lo_set")
        y_done, y_set, stored = sem("y_done"), sem("y_set"), sem("stored")

        WARM_UP = 8
        LN = 9
        LN_VAR = 5

        block = ctx.enter_context(nc.Block())

        @block.sync
        def _(sp):
            sp.dma_start(alpha_sb[:], alpha.rearrange("(p t) -> p t", t=T)).then_inc(alpha_in, 16)
            sp.dma_start(adj_sb[:, 0, :], adj_dram[0]).then_inc(adj_in[0], 16)
            sp.dma_start(w_sb[:], w).then_inc(w_in, 16)
            sp.dma_start(adj_sb[:, 1, :], adj_dram[1]).then_inc(adj_in[1], 16)
            sp.dma_start(d_sb[:], d.rearrange("(p o) -> p o", o=1)).then_inc(d_in, 16)
            for t in range(2, T):
                sp.dma_start(adj_sb[:, t, :], adj_dram[t]).then_inc(adj_in[t], 16)
            for j in range(GB):
                sp.dma_start(xs[:, j, :, :], x_dram[j]).then_inc(x_in[j], 16)
            with sp.Fori(1, G) as g:
                for j in range(GB):
                    sp.wait_ge(x_in[j], 16 * g)
                    sp.dma_start(xs[:, bass.ds(GB * g + j, 1), :, :],
                                 x_dram[bass.ds(GB * g + j, 1)].rearrange("o p n -> (o p) n")).then_inc(x_in[j], 16)
            with sp.Fori(0, G) as g:
                for t in range(T):
                    sp.wait_ge(y_set, T * g + t + 1)
                    sp.dma_start(out_dram[bass.ds(g, 1), t].rearrange("o p b d -> (o p) b d"),
                                 xs[:, bass.ds(GB * g, GB), t, :]).then_inc(stored, 16)
            sp.wait_ge(stored, 16 * G * T)

        @block.gpsimd
        def _(pool):
            nc.gpsimd.memset(ident[:], 0.0).then_inc(zeros_set, 1)
            pool.wait_ge(zeros_set, 1)
            nc.gpsimd.affine_select(out=ident[:], in_=ident[:], compare_op=ALU.not_equal, fill=1.0, base=0,
                                    pattern=[[-1, P]], channel_multiplier=1).then_inc(ident_set, 1)
            pool.wait_ge(ident_set, 1)
            nc.gpsimd.tensor_copy(R[:, STEPS, :], ident[:]).then_inc(r0_set, 1)
            for k in range(STEPS + 1):
                ins = nc.gpsimd.memset(binom[:, k:k + 1], float(comb(STEPS, k)))
            ins.then_inc(binom_set, 1)
            for t in range(T):
                pool.wait_ge(L_hi_set, t + 1)
                nc.gpsimd.tensor_tensor(L_lo[:, t], L[:, t], L_hi[:, t].bitcast(F32), ALU.subtract).then_inc(L_lo_set, 1)

            pool.wait_ge(R_set, 4)
            pool.wait_ge(b_in, 16)
            pool.wait_ge(L_set, T)
            nc.gpsimd.tensor_tensor(g_terms, R[:], b_rows[:].rearrange("p (o n) -> p o n", o=1)
                                    .to_broadcast([P, STEPS + 1, P]), ALU.mult).then_inc(g_terms_set, 1)

            def group(g):
                for j in range(GB):
                    pool.wait_ge(c_lo_set, 2 * (GB * g + j) + 2)
                    xb = xs[:, bass.ds(GB * g + j, 1), :, :].rearrange("p o t d -> p (o t d)")
                    nc.gpsimd.tensor_tensor(xb, xb, bias[:], ALU.add).then_inc(bias_added, 1)

            pool.wait_ge(bias_set, 1)
            with pool.Fori(0, G) as g:
                group(g)

        @block.scalar
        def _(act):
            act.wait_ge(ones_set, 1)
            nc.scalar.activation(unused[:, 0:1], ones[:], ACT.Exp)
            act.dma_start(fc_sb[:], fc_w).then_inc(fc_in, 16)
            act.dma_start(b_rows[:], fc_b.partition_broadcast(P)).then_inc(b_in, 16)
            act.wait_ge(alpha_in, 16)
            nc.scalar.activation(exp_alpha[:], alpha_sb[:], ACT.Exp, scale=-1.0).then_inc(exp_set, 1)
            nc.scalar.activation(unused[:, 1:2], ones[:], ACT.Sqrt)

            def power_of_r(n, lo, hi):
                act.wait_ge(R_done, n)
                nc.scalar.activation(R[:, lo:hi, :], psS[:, 0:(hi - lo) * P], ACT.Copy).then_inc(R_set, 1)

            def split_L(t):
                act.wait_ge(L_set, t + 1)
                nc.scalar.activation(L_hi[:, t], L[:, t], ACT.Copy).then_inc(L_hi_set, 1)

            def power_hi(done, count, hi, hi_set, t):
                act.wait_ge(done, count)
                nc.scalar.activation(hi[:, t, :], psW[:, t, :], ACT.Copy).then_inc(hi_set, 1)

            def fr_scaled(n):
                act.wait_ge(FR_done, n + 1)
                for k in range(3 * n, 3 * n + 3):
                    s, c = place[k]
                    ins = nc.scalar.activation(C[:, s, c * P:(c + 1) * P], psS[:, (k - 3 * n) * P:(k - 3 * n + 1) * P],
                                               ACT.Copy, scale=float(comb(STEPS, k)))
                ins.then_inc(FR_set, 1)

            def deviation(i):
                act.wait_ge(ln_chain, LN * i + LN_VAR)
                nc.scalar.activation(std[:], var_eps[:], ACT.Sqrt).then_inc(std_set, 1)

            def x0_hi(i, n):
                act.wait_ge(normed_set, i + 1)
                if not (isinstance(i, int) and i < 2):
                    act.wait_ge(z_done, 2 * i - 2)
                nc.scalar.activation(x0[n][0][:], normed[n][:], ACT.Relu).then_inc(x0_hi_set, 1)

            def xT_hi(i, n):
                act.wait_ge(xT_done, i + 1)
                nc.scalar.activation(srcT[n][0][0][:], psT[:], ACT.Relu).then_inc(xT_hi_set, 1)

            def z_hi(i, n, s):
                act.wait_ge(z_done, 2 * i + s)
                nc.scalar.activation(srcT[n][s][0][:], psZ[:, s - 1, :], ACT.Copy).then_inc(z_hi_set, 1)

            def c_hi(i, j):
                for h in range(2):
                    act.wait_ge(c_done, 2 * i + h + 1)
                    nc.scalar.activation(q2_hi[:, 2 * h:2 * h + 2, j, :], psW[:, 2 * h:2 * h + 2, 0:P], ACT.Copy)
                    nc.scalar.activation(r1[:, 2 * h:2 * h + 2, j, :], psW[:, 2 * h:2 * h + 2, P:2 * P],
                                         ACT.Copy).then_inc(c_hi_set, 1)

            def y1_hi_part(g):
                for t in range(T):
                    act.wait_ge(y1_sum_set, T * g + t + 1)
                    nc.scalar.activation(y1_hi[:, t], y1_sum[t % 2][:], ACT.Copy).then_inc(y1_hi_set, 1)

            def group(g, last=False):
                xT_hi(GB * g + 2, 0)
                z_hi(GB * g + 2, 0, 1)
                z_hi(GB * g + 2, 0, 2)
                c_hi(GB * g + 1, 1)
                xT_hi(GB * g + 3, 1)
                z_hi(GB * g + 3, 1, 1)
                z_hi(GB * g + 3, 1, 2)
                if not last:
                    deviation(GB * g + 4)
                c_hi(GB * g + 2, 2)
                if not last:
                    x0_hi(GB * g + 4, 0)
                    deviation(GB * g + 5)
                c_hi(GB * g + 3, 3)
                if not last:
                    x0_hi(GB * g + 5, 1)
                    deviation(GB * g + 6)
                    xT_hi(GB * g + 4, 0)
                    z_hi(GB * g + 4, 0, 1)
                    z_hi(GB * g + 4, 0, 2)
                    x0_hi(GB * g + 6, 0)
                    deviation(GB * g + 7)
                y1_hi_part(g)
                if not last:
                    xT_hi(GB * g + 5, 1)
                    z_hi(GB * g + 5, 1, 1)
                    z_hi(GB * g + 5, 1, 2)
                    x0_hi(GB * g + 7, 1)
                    c_hi(GB * g + 4, 0)

            split_L(0)
            power_of_r(1, 7, 8)
            split_L(1)
            split_L(2)
            power_of_r(2, 6, 7)
            split_L(3)
            for t in range(T):
                power_hi(LT_done, 1, LT_hi, LT_hi_set, t)
            power_of_r(3, 4, 6)
            deviation(0)
            x0_hi(0, 0)
            power_hi(L2T_done, 1, L2T_hi, L2T_hi_set, 0)
            power_of_r(4, 0, 4)
            power_hi(L2T_done, 2, L2T_hi, L2T_hi_set, 1)
            fr_scaled(0)
            deviation(1)
            power_hi(L2T_done, 3, L2T_hi, L2T_hi_set, 2)
            fr_scaled(1)
            power_hi(L2T_done, 4, L2T_hi, L2T_hi_set, 3)
            x0_hi(1, 1)
            fr_scaled(2)
            xT_hi(0, 0)
            z_hi(0, 0, 1)
            for t in range(T):
                power_hi(L3T_done, t + 1, L3T_hi, L3T_hi_set, t)
            act.wait_ge(C_sum, STEPS)
            nc.scalar.activation(C_hi[:], C[:], ACT.Copy).then_inc(C_hi_set, 1)
            deviation(2)
            z_hi(0, 0, 2)
            xT_hi(1, 1)
            z_hi(1, 1, 1)
            x0_hi(2, 0)
            z_hi(1, 1, 2)
            deviation(3)
            x0_hi(3, 1)
            c_hi(0, 0)
            with act.Fori(0, G - 1) as g:
                group(g)
            group(G - 1, last=True)

        @block.tensor
        def _(pe):
            def product(o, a, b, start, stop):
                nc.tensor.matmul(o, a[0], b[0], start=start, stop=False)
                nc.tensor.matmul(o, a[0], b[1], start=False, stop=False)
                return nc.tensor.matmul(o, a[1], b[0], start=False, stop=stop)

            def power_tile(b_hi, b_lo, t):
                for k in range(T):
                    ins = product(psW[:, t, :], (L_hi[:, k, t, :], L_lo[:, k, t, :]), (b_hi[:, k, :], b_lo[:, k, :]),
                                  k == 0, k == T - 1)
                return ins

            def transpose_x(i, n):
                pe.wait_ge(normed_set, i + 1)
                if not (isinstance(i, int) and i < 1):
                    pe.wait_ge(xT_lo_set, i)
                for t in range(T):
                    ins = nc.tensor.transpose(psT[:, t * P:(t + 1) * P], normed[n][:, t, :], ident[:])
                ins.then_inc(xT_done, 1)

            def make_z(i, n, s):
                if s == 1:
                    pe.wait_ge(x0_lo_set, i + 1)
                if not (isinstance(i, int) and i < 1):
                    pe.wait_ge(z_lo_set, 2 * i - 2 + s)
                lsT_hi, lsT_lo = (LT_hi, LT_lo) if s == 1 else (L2T_hi, L2T_lo)
                for m in range(T):
                    ins = product(psZ[:, s - 1, :], (x0[n][0][:, m, :], x0[n][1][:, m, :]),
                                  (lsT_hi[:, m, :], lsT_lo[:, m, :]), m == 0, m == T - 1)
                ins.then_inc(z_done, 1)

            def make_c(i, j, n):
                pe.wait_ge(xT_lo_set, i + 1)
                pe.wait_ge(z_lo_set, 2 * i + 2)
                for t in range(T):
                    if t % 2 == 0 and j > 0:
                        pe.wait_ge(c_lo_set, 2 * i - 1 + t // 2)
                    if t % 2 == 0 and j == 0 and not (isinstance(i, int) and i == 0):
                        pe.wait_ge(y_set, i - 2 + t)
                    nodes = slice(t * P, (t + 1) * P)
                    for s in range(3):
                        ins = product(psW[:, t, 0:3 * P], (srcT[n][s][0][:, nodes], srcT[n][s][1][:, nodes]),
                                      (C_hi[:, s, :], C_lo[:, s, :]), s == 0, s == 2)
                    if t % 2 == 1:
                        ins.then_inc(c_done, 1)

            def make_y1(g):
                for t in range(T):
                    if t % 2 == 0:
                        pe.wait_ge(c_lo_set, 2 * GB * g + 2 * GB - 1 + t // 2)
                    nodes = slice(t * P, (t + 1) * P)
                    for m in range(T):
                        if t == 0 and m % 2 == 0:
                            pe.wait_ge(q2_lo_set, 2 * GB * g + 2 * GB - 1 + m // 2)
                        ins = product(psW[:, t, :], (L3T_hi[:, m, nodes], L3T_lo[:, m, nodes]),
                                      (q2_hi[:, m], q2_lo[:, m]), m == 0, m == T - 1)
                    ins.then_inc(y1_done, 1)

            def make_y(g):
                for t in range(T):
                    nodes = slice(t * P, (t + 1) * P)
                    for m in range(T):
                        if t == 0:
                            pe.wait_ge(y1_lo_set, T * g + m + 1)
                        ins = product(psW[:, t, :], (L3T_hi[:, m, nodes], L3T_lo[:, m, nodes]),
                                      (y1_hi[:, m], y1_lo[:, m]), m == 0, m == T - 1)
                    ins.then_inc(y_done, 1)

            def group(g, last=False):
                transpose_x(GB * g + 2, 0)
                make_z(GB * g + 2, 0, 1)
                make_z(GB * g + 2, 0, 2)
                make_c(GB * g + 1, 1, 1)
                transpose_x(GB * g + 3, 1)
                make_z(GB * g + 3, 1, 1)
                make_z(GB * g + 3, 1, 2)
                make_c(GB * g + 2, 2, 0)
                make_c(GB * g + 3, 3, 1)
                if not last:
                    transpose_x(GB * g + 4, 0)
                    make_z(GB * g + 4, 0, 1)
                    make_z(GB * g + 4, 0, 2)
                make_y1(g)
                if not last:
                    transpose_x(GB * g + 5, 1)
                    make_z(GB * g + 5, 1, 1)
                    make_z(GB * g + 5, 1, 2)
                make_y(g)
                if not last:
                    make_c(GB * g + 4, 0, 0)

            def u_times(b_hi, b_lo):
                for n, (b, m) in enumerate([(b, m) for b in (b_hi, b_lo) for m in range(T)]):
                    ins = nc.tensor.matmul(psS[:], u_split[:, m, :], b[:, m, :], start=(n == 0), stop=(n == 2 * T - 1))
                ins.then_inc(u_rows_done, 1)

            def u_columns():
                for t in range(T):
                    ins = nc.tensor.transpose(psS[:, t * P:(t + 1) * P], u_rows[:, t * P:(t + 1) * P], ident[:])
                ins.then_inc(u_cols_done, 1)

            def power_of_r(n, by, lo, hi):
                pe.wait_ge(R_set, n)
                nc.tensor.matmul(psS[:, 0:(hi + 1 - lo) * P], R[:, STEPS - by, :],
                                 R[:, STEPS - hi:STEPS + 1 - lo, :], start=True, stop=True).then_inc(R_done, 1)

            def transpose_l(t):
                pe.wait_ge(L_set, t + 1)
                for m in range(T):
                    ins = nc.tensor.transpose(psW[:, m, t * P:(t + 1) * P], L[:, t, m, :], ident[:])
                if t == T - 1:
                    ins.then_inc(LT_done, 1)

            pe.wait_ge(ident_set, 1)
            for _ in range(WARM_UP):
                nc.tensor.matmul(psZ[:, 0, 0:P], ident[:], ident[:], start=True, stop=True)
            pe.wait_ge(w_in, 16)
            nc.tensor.transpose(psS[:, 0:P], w_sb[:], ident[:]).then_inc(wT_done, 1)
            transpose_l(0)
            pe.wait_ge(wTd_set, 1)
            nc.tensor.matmul(psS[:, 0:P], wTd[:], wT[:], start=True, stop=True).then_inc(R_done, 1)
            transpose_l(1)
            transpose_l(2)
            power_of_r(1, 1, 1, 1)
            transpose_l(3)
            power_of_r(2, 2, 1, 2)
            for k in range(T):
                pe.wait_ge(L_lo_set, k + 1)
                pe.wait_ge(LT_lo_set, k + 1)
                ins = product(psW[:, 0, :], (L_hi[:, k, 0, :], L_lo[:, k, 0, :]), (LT_hi[:, k, :], LT_lo[:, k, :]),
                              k == 0, k == T - 1)
            ins.then_inc(L2T_done, 1)
            power_of_r(3, 4, 1, 4)
            power_tile(LT_hi, LT_lo, 1).then_inc(L2T_done, 1)
            pe.wait_ge(fc_in, 16)
            pe.wait_ge(R_set, 4)
            pe.wait_ge(r0_set, 1)
            for n in range(3):
                if n:
                    power_tile(LT_hi, LT_lo, n + 1).then_inc(L2T_done, 1)
                    pe.wait_ge(FR_set, n)
                nc.tensor.matmul(psS[:, 0:3 * P], fc_sb[:], R[:, 3 * n:3 * n + 3, :], start=True,
                                 stop=True).then_inc(FR_done, 1)
            transpose_x(0, 0)
            make_z(0, 0, 1)
            pe.wait_ge(L2T_lo_set, T)
            power_tile(L2T_hi, L2T_lo, 0).then_inc(L3T_done, 1)
            pe.wait_ge(FR_set, 3)
            pe.wait_ge(u_split_set, 1)
            u_times(LT_hi, LT_lo)
            power_tile(L2T_hi, L2T_lo, 1).then_inc(L3T_done, 1)
            pe.wait_ge(u_rows_set, 1)
            pe.wait_ge(g_set, 1)
            nc.tensor.transpose(psS[:, 0:P], g_col[:], ident[:]).then_inc(g_rows_done, 1)
            power_tile(L2T_hi, L2T_lo, 2).then_inc(L3T_done, 1)
            pe.wait_ge(g_rows_set, 1)
            u_columns()
            power_tile(L2T_hi, L2T_lo, 3).then_inc(L3T_done, 1)
            pe.wait_ge(u_split_set, 2)
            for t in range(T):
                ins = nc.tensor.transpose(psS[:, t * P:(t + 1) * P], u_split[:, t, :].bitcast(F32), ident[:])
            ins.then_inc(u_rows_done, 1)
            make_z(0, 0, 2)
            pe.wait_ge(u_rows_set, 2)
            pe.wait_ge(L3T_lo_set, T)
            u_times(L3T_hi, L3T_lo)
            transpose_x(1, 1)
            make_z(1, 1, 1)
            pe.wait_ge(u_rows_set, 3)
            u_columns()
            make_z(1, 1, 2)
            pe.wait_ge(u_split_set, 3)
            u_times(L3T_hi, L3T_lo)
            pe.wait_ge(C_lo_set, 1)
            make_c(0, 0, 0)
            pe.wait_ge(u_rows_set, 4)
            for t in range(T):
                ins = nc.tensor.matmul(psS[:, t * P:(t + 1) * P], u_rows[:, t * P:(t + 1) * P], g_rows[:],
                                       start=True, stop=True)
            ins.then_inc(bias_done, 1)
            with pe.Fori(0, G - 1) as g:
                group(g)
            group(G - 1, last=True)

        @block.vector
        def _(dve):
            def lo_part(lo, full, hi):
                return nc.vector.tensor_tensor(lo, full, hi.bitcast(F32), ALU.subtract)

            def power_lo(hi_set, hi, lo, lo_set, t):
                dve.wait_ge(hi_set, t + 1)
                lo_part(lo[:, t, :], psW[:, t, :], hi[:, t, :]).then_inc(lo_set, 1)

            def statistics(i, j, g):
                dve.wait_ge(x_in[j], 16 * g + 16)
                xb = xs[:, bass.ds(i, 1), :, :]
                for t in range(T):
                    ins = nc.vector.bn_stats(stats[:, t, :], xb[:, :, t, :].rearrange("p o d -> p (o d)"))
                ins.then_inc(ln_chain, 1)
                dve.wait_ge(ln_chain, LN * i + 1)
                nc.vector.tensor_tensor(halves[:], stats[:, :, 1:3], stats[:, :, 4:6], ALU.add)
                nc.vector.tensor_tensor(halves_apart[:], stats[:, :, 1], stats[:, :, 4],
                                        ALU.subtract).then_inc(ln_chain, 1)
                dve.wait_ge(ln_chain, LN * i + 2)
                nc.vector.tensor_scalar(mean[:], halves[:, :, 0], 0.5, None, ALU.mult)
                nc.vector.tensor_tensor(apart_sq[:], halves_apart[:], halves_apart[:], ALU.mult).then_inc(ln_chain, 1)
                dve.wait_ge(ln_chain, LN * i + 3)
                nc.vector.scalar_tensor_tensor(apart_sq[:], apart_sq[:], D / 4.0, halves[:, :, 1], ALU.mult,
                                               ALU.add).then_inc(ln_chain, 1)
                dve.wait_ge(ln_chain, LN * i + 4)
                nc.vector.tensor_scalar(var_eps[:], apart_sq[:], 1.0 / D, EPS, ALU.mult, ALU.add).then_inc(ln_chain, 1)

            def normalize(i, n):
                dve.wait_ge(std_set, i + 1)
                nc.vector.reciprocal(rstd0[:], std[:]).then_inc(ln_chain, 1)
                dve.wait_ge(ln_chain, LN * i + 6)
                nc.vector.tensor_tensor(newton[:], var_eps[:], rstd0[:], ALU.mult).then_inc(ln_chain, 1)
                dve.wait_ge(ln_chain, LN * i + 7)
                nc.vector.scalar_tensor_tensor(newton[:], newton[:], -0.5, rstd0[:], ALU.mult, ALU.mult).then_inc(ln_chain, 1)
                dve.wait_ge(ln_chain, LN * i + 8)
                nc.vector.scalar_tensor_tensor(rstd[:], newton[:], 1.5, rstd0[:], ALU.add, ALU.mult).then_inc(ln_chain, 1)
                dve.wait_ge(ln_chain, LN * i + 9)
                xb = xs[:, bass.ds(i, 1), :, :]
                if not (isinstance(i, int) and i < 2):
                    dve.wait_ge(xT_done, i - 1)
                    dve.wait_ge(x0_hi_set, i - 1)
                for t in range(T):
                    ins = nc.vector.tensor_scalar(normed[n][:, t, :], xb[:, :, t, :].rearrange("p o d -> p (o d)"),
                                                  mean[:, t:t + 1], rstd[:, t:t + 1], ALU.subtract, ALU.mult)
                ins.then_inc(normed_set, 1)

            def relu_lo(lo, full, hi):
                return nc.vector.scalar_tensor_tensor(lo, full, 0.0, hi.bitcast(F32), ALU.max, ALU.subtract)

            def x0_lo(i, n):
                dve.wait_ge(x0_hi_set, i + 1)
                relu_lo(x0[n][1][:], normed[n][:], x0[n][0][:]).then_inc(x0_lo_set, 1)

            def xT_lo(i, n):
                dve.wait_ge(xT_hi_set, i + 1)
                relu_lo(srcT[n][0][1][:], psT[:], srcT[n][0][0][:]).then_inc(xT_lo_set, 1)

            def z_lo(i, n, s):
                dve.wait_ge(z_hi_set, 2 * i + s)
                lo_part(srcT[n][s][1][:], psZ[:, s - 1, :], srcT[n][s][0][:]).then_inc(z_lo_set, 1)

            def c_lo(i, j):
                for h in range(2):
                    dve.wait_ge(c_hi_set, 2 * i + h + 1)
                    t2 = slice(2 * h, 2 * h + 2)
                    lo_part(q2_lo[:, t2, j, :], psW[:, t2, 0:P], q2_hi[:, t2, j, :]).then_inc(q2_lo_set, 1)
                    xb = xs[:, bass.ds(i, 1), t2, :].rearrange("p o t d -> p (o t) d")
                    nc.vector.tensor_tensor(xb, psW[:, t2, 2 * P:3 * P], xb, ALU.add).then_inc(c_lo_set, 1)

            def y1_lo_tile(g, t):
                dve.wait_ge(y1_hi_set, T * g + t + 1)
                lo_part(y1_lo[:, t], y1_sum[t % 2][:], y1_hi[:, t]).then_inc(y1_lo_set, 1)

            def y1_part(g):
                for t in range(T):
                    dve.wait_ge(y1_done, T * g + t + 1)
                    if t >= 2:
                        dve.wait_ge(y1_lo_set, T * g + t - 1)
                    nc.vector.tensor_tensor(y1_sum[t % 2][:], psW[:, t, :], r1[:, t].rearrange("p b d -> p (b d)"),
                                            ALU.add).then_inc(y1_sum_set, 1)
                    if t:
                        y1_lo_tile(g, t - 1)
                y1_lo_tile(g, T - 1)

            def y_part(g):
                dve.wait_ge(bias_added, GB * g + GB)
                for t in range(T):
                    dve.wait_ge(y_done, T * g + t + 1)
                    xg = xs[:, bass.ds(GB * g, GB), t, :]
                    nc.vector.tensor_tensor(xg, psW[:, t, :].rearrange("p (b d) -> p b d", b=GB), xg,
                                            ALU.add).then_inc(y_set, 1)

            def group(g, last=False):
                xT_lo(GB * g + 2, 0)
                z_lo(GB * g + 2, 0, 1)
                z_lo(GB * g + 2, 0, 2)
                c_lo(GB * g + 1, 1)
                xT_lo(GB * g + 3, 1)
                z_lo(GB * g + 3, 1, 1)
                z_lo(GB * g + 3, 1, 2)
                if not last:
                    statistics(GB * g + 4, 0, g + 1)
                c_lo(GB * g + 2, 2)
                if not last:
                    normalize(GB * g + 4, 0)
                    statistics(GB * g + 5, 1, g + 1)
                    x0_lo(GB * g + 4, 0)
                c_lo(GB * g + 3, 3)
                if not last:
                    normalize(GB * g + 5, 1)
                    statistics(GB * g + 6, 2, g + 1)
                    x0_lo(GB * g + 5, 1)
                    xT_lo(GB * g + 4, 0)
                    z_lo(GB * g + 4, 0, 1)
                    z_lo(GB * g + 4, 0, 2)
                    normalize(GB * g + 6, 0)
                    statistics(GB * g + 7, 3, g + 1)
                    x0_lo(GB * g + 6, 0)
                y1_part(g)
                if not last:
                    xT_lo(GB * g + 5, 1)
                    z_lo(GB * g + 5, 1, 1)
                    z_lo(GB * g + 5, 1, 2)
                    normalize(GB * g + 7, 1)
                    x0_lo(GB * g + 7, 1)
                y_part(g)
                if not last:
                    c_lo(GB * g + 4, 0)

            def split_u(n, block_u):
                dve.wait_ge(u_chain, n)
                o = 32 * block_u
                nc.vector.tensor_copy(u_split[:, :, o:o + 3], u_col[:]).then_inc(u_chain, 1)
                dve.wait_ge(u_chain, n + 1)
                lo_part(u_split[:, :, o + 3:o + 6], u_col[:], u_split[:, :, o:o + 3]).then_inc(u_split_set, 1)

            def add_u_columns(n, lo, hi, first):
                dve.wait_ge(u_chain, n)
                columns = psS[:].rearrange("p (t c) -> p t c", c=P)[:, :, 32 + first:32 + first + 3 + hi - lo]
                nc.vector.tensor_copy(u_col[:, :, lo:hi], columns[:, :, 0:hi - lo]).then_inc(u_chain, 1)
                dve.wait_ge(u_chain, n + 1)
                nc.vector.tensor_tensor(u_col[:, :, lo:hi], columns[:, :, 3:3 + hi - lo], u_col[:, :, lo:hi],
                                        ALU.add).then_inc(u_chain, 1)

            def keep_u_rows(done, block_to, block_from):
                dve.wait_ge(u_rows_done, done)
                to, fr = 32 * block_to, 32 * block_from
                nc.vector.tensor_copy(u_rows[to:to + 6, :], psS[fr:fr + 6, :]).then_inc(u_rows_set, 1)

            def make_l(t):
                dve.wait_ge(adj_in[t], 16)
                nc.vector.tensor_scalar(L[:, t], adj_sb[:, t, :].rearrange("p (q c) -> p c q", c=T), gate[:, t:t + 1],
                                        None, ALU.mult).then_inc(L_scaled, 1)
                dve.wait_ge(L_scaled, t + 1)
                nc.vector.scalar_tensor_tensor(L[:, t, t, :], ident[:], diag[:, t:t + 1], L[:, t, t, :], ALU.mult,
                                               ALU.add).then_inc(L_set, 1)

            def polynomial(i):
                if i:
                    dve.wait_ge(C_sum, i)
                for k in range(STEPS - i):
                    s, c = place[k]
                    block_k = C[:, s, c * P:(c + 1) * P]
                    ins = nc.vector.scalar_tensor_tensor(block_k, R[:, STEPS - i, :], DT * comb(k + i, k), block_k,
                                                         ALU.mult, ALU.add)
                ins.then_inc(C_sum, 1)

            nc.vector.memset(ones[:], 1.0).then_inc(ones_set, 1)
            nc.vector.memset(u_split[:].bitcast(F32), 0.0).then_inc(u_zero, 1)
            nc.vector.memset(u_rows[:], 0.0).then_inc(u_zero, 1)
            nc.vector.memset(g_col[:], 0.0).then_inc(u_zero, 1)
            nc.vector.memset(u_col[:], 1.0).then_inc(u_chain, 1)
            dve.wait_ge(exp_set, 1)
            nc.vector.tensor_scalar(exp_alpha[:], exp_alpha[:], 1.0, None, ALU.add).then_inc(gate_chain, 1)
            dve.wait_ge(gate_chain, 1)
            nc.vector.reciprocal(gate[:], exp_alpha[:]).then_inc(gate_chain, 1)
            dve.wait_ge(gate_chain, 2)
            nc.vector.tensor_scalar(gate[:], gate[:], DT * 0.5, None, ALU.mult).then_inc(gate_chain, 1)
            dve.wait_ge(gate_chain, 3)
            nc.vector.tensor_scalar(diag[:], gate[:], -1.0, 1.0 - DT, ALU.mult, ALU.add).then_inc(gate_set, 1)
            dve.wait_ge(gate_set, 1)
            dve.wait_ge(ident_set, 1)
            make_l(0)
            dve.wait_ge(d_in, 16)
            nc.vector.tensor_scalar(d_clip[:], d_sb[:], 0.0, 1.0, ALU.max, ALU.min).then_inc(d_set, 1)
            dve.wait_ge(wT_done, 1)
            nc.vector.tensor_copy(wT[:], psS[:, 0:P])
            dve.wait_ge(d_set, 1)
            nc.vector.tensor_scalar(wTd[:], psS[:, 0:P], d_clip[:, 0:1], DT, ALU.mult, ALU.mult).then_inc(wTd_set, 1)
            for t in range(1, T):
                make_l(t)
            statistics(0, 0, 0)
            for t in range(T):
                power_lo(LT_hi_set, LT_hi, LT_lo, LT_lo_set, t)
            normalize(0, 0)
            statistics(1, 1, 0)
            x0_lo(0, 0)
            dve.wait_ge(u_chain, 1)
            nc.vector.tensor_reduce(u_col[:, :, 1], L[:].rearrange("p t c q -> p t (c q)"), AX.X,
                                    ALU.add).then_inc(u_chain, 1)
            dve.wait_ge(u_zero, 3)
            split_u(2, 1)
            power_lo(L2T_hi_set, L2T_hi, L2T_lo, L2T_lo_set, 0)
            power_lo(L2T_hi_set, L2T_hi, L2T_lo, L2T_lo_set, 1)
            normalize(1, 1)
            statistics(2, 2, 0)
            power_lo(L2T_hi_set, L2T_hi, L2T_lo, L2T_lo_set, 2)
            power_lo(L2T_hi_set, L2T_hi, L2T_lo, L2T_lo_set, 3)
            x0_lo(1, 1)
            dve.wait_ge(FR_set, 3)
            dve.wait_ge(r0_set, 1)
            polynomial(0)
            polynomial(1)
            dve.wait_ge(g_terms_set, 1)
            nc.vector.tensor_reduce(g_raw[:], g_terms, AX.X, ALU.add).then_inc(g_raw_set, 1)
            dve.wait_ge(g_raw_set, 1)
            dve.wait_ge(binom_set, 1)
            blocks = g_col[:, 0:3 * 32].rearrange("p (n c) -> p n c", c=32)
            for o in (0, 3):
                ins = nc.vector.tensor_tensor(blocks[:, :, o:o + 3], g_raw[:].rearrange("p (n c) -> p n c", c=3),
                                              binom[:].rearrange("p (n c) -> p n c", c=3), ALU.mult)
            ins.then_inc(g_set, 1)
            xT_lo(0, 0)
            z_lo(0, 0, 1)
            polynomial(2)
            power_lo(L3T_hi_set, L3T_hi, L3T_lo, L3T_lo_set, 0)
            keep_u_rows(1, 1, 1)
            polynomial(3)
            power_lo(L3T_hi_set, L3T_hi, L3T_lo, L3T_lo_set, 1)
            dve.wait_ge(g_rows_done, 1)
            nc.vector.tensor_copy(g_rows[:], psS[:, 0:P]).then_inc(g_rows_set, 1)
            polynomial(4)
            power_lo(L3T_hi_set, L3T_hi, L3T_lo, L3T_lo_set, 2)
            dve.wait_ge(u_cols_done, 1)
            add_u_columns(3, 2, 3, 1)
            split_u(5, 1)
            for i in range(5, STEPS):
                polynomial(i)
            power_lo(L3T_hi_set, L3T_hi, L3T_lo, L3T_lo_set, 3)
            keep_u_rows(2, 0, 1)
            dve.wait_ge(C_hi_set, 1)
            lo_part(C_lo[:], C[:], C_hi[:]).then_inc(C_lo_set, 1)
            z_lo(0, 0, 2)
            keep_u_rows(3, 1, 1)
            xT_lo(1, 1)
            z_lo(1, 1, 1)
            dve.wait_ge(u_cols_done, 2)
            add_u_columns(6, 0, 3, 0)
            split_u(8, 2)
            normalize(2, 0)
            statistics(3, 3, 0)
            z_lo(1, 1, 2)
            x0_lo(2, 0)
            keep_u_rows(4, 2, 2)
            normalize(3, 1)
            x0_lo(3, 1)
            c_lo(0, 0)
            dve.wait_ge(bias_done, 1)
            nc.vector.tensor_copy(bias[:], psS[:]).then_inc(bias_set, 1)
            with dve.Fori(0, G - 1) as g:
                group(g)
            group(G - 1, last=True)


_INS = ["x", "adj", "L0_gnn_alpha_train", "L0_gnn_w", "L0_gnn_d", "L0_gnn_fc_in_w", "L0_gnn_fc_in_b"]


def kernel(**inputs):
    import numpy as np
    import concourse.bacc as bacc
    from concourse.bass_utils import run_bass_kernel_spmd

    nc = bacc.Bacc("TRN2", target_bir_lowering=False, num_devices=1)
    arrays, args = {}, []
    for name in _INS:
        a = np.ascontiguousarray(inputs[name])
        arrays[f"in_{name}"] = a
        args.append(nc.dram_tensor(f"in_{name}", a.shape, mybir.dt.from_np(a.dtype), kind="ExternalInput").ap())
    args.append(nc.dram_tensor("out_0", arrays["in_x"].shape, F32, kind="ExternalOutput").ap())
    build(nc, *args)
    r = run_bass_kernel_spmd(nc, [arrays], core_ids=[0])
    return r.results[0]["out_0"]
```
